# Optimizing a Trainium2 kernel written in Bass

```python
import numpy as np
import jax
import jax.numpy as jnp

def _softmax(x, axis=-1):
    return jax.nn.softmax(x, axis=axis)

def _gelu(x):
    return jax.nn.gelu(x, approximate=True)

def _silu(x):
    return jax.nn.silu(x)

def _sigmoid(x):
    return jax.nn.sigmoid(x)

def _layernorm(x, axis=-1, eps=1e-05):
    m = jnp.mean(x, axis=axis, keepdims=True)
    v = jnp.var(x, axis=axis, keepdims=True)
    return (x - m) / jnp.sqrt(v + eps)

def _scatter_add(tgt, idx, src, axis=0):
    return tgt.at[idx].add(src)

def _segment_sum(src, seg, n):
    return jax.ops.segment_sum(src, seg, n)
kernel_name = 'mk_xattn_seq_d2_seqx_r8_ed78bd'

def setup_inputs(seed: int=0):
    np.random.seed(seed)
    _w = jnp.asarray

    def _rec_inputs():
        import jax
        import jax.numpy as jnp
        _rk = jax.random.key(seed)
        x = 7.22e-05 + 1 * jax.random.normal(jax.random.fold_in(_rk, 1), (8, 128, 256), jnp.float32)
        _lenS = 128 - jax.random.randint(jax.random.fold_in(_rk, 7), (8,), 0, max(1, 128 // 4) + 1, jnp.int32)
        _lenS2 = 128 - jax.random.randint(jax.random.fold_in(_rk, 8), (8,), 0, max(1, 128 // 4) + 1, jnp.int32)
        _ctx_2048P = jax.random.normal(jax.random.fold_in(_rk, 11), (8, 16, 256), jnp.float32)
        _ctx_2048c = jax.random.dirichlet(jax.random.fold_in(_rk, 511), 0.3 * jnp.ones((16,), jnp.float32), (8, 128))
        _ctx_2048t = jnp.einsum('bsk,bkd->bsd', _ctx_2048c, _ctx_2048P)
        _ctx_2048t = _ctx_2048t * jax.lax.rsqrt(jnp.mean(jnp.square(_ctx_2048t)) + 1e-12) * 0.953939
        ctx_2048 = 2.81802e-05 + 1.00001 * (_ctx_2048t + 0.3 * jax.random.normal(jax.random.fold_in(_rk, 611), (8, 128, 256), jnp.float32))
        _validS = jnp.arange(128)[None, :] < _lenS[:, None]
        _validS2 = jnp.arange(128)[None, :] < _lenS2[:, None]
        _causal = jnp.tril(jnp.ones((128, 128), dtype=bool))
        mask_BxS2_bf1 = jnp.ones((8, 128), dtype=bool)
        mask_BxS2_ik0 = jnp.where(jnp.broadcast_to(_validS2[:, :], (8, 128)), 0, 1).astype(jnp.int32)
        return (x, ctx_2048, mask_BxS2_bf1, mask_BxS2_ik0)
    x, ctx_2048, mask_BxS2_bf1, mask_BxS2_ik0 = _rec_inputs()

    def _L0_xattn_setup():
        import jax, jax.numpy as jnp
        import numpy as np
        D = 256
        H = 16
        HD = D // H
        INNER = 4 * D
        EPS = 1e-05

        def layer_norm(x, w, b):
            mu = jnp.mean(x, axis=-1, keepdims=True)
            var = jnp.mean(jnp.square(x - mu), axis=-1, keepdims=True)
            return (x - mu) * jax.lax.rsqrt(var + EPS) * w + b
        key = jax.random.key(seed)
        ks = jax.random.split(key, 12)
        B, LQ, LK = (4, 128, 256)
        std = 0.02
        inp = {'hidden_states': jax.random.normal(ks[0], (B, LQ, D), jnp.float32), 'encoder_hidden_states': jax.random.normal(ks[1], (B, LK, D), jnp.float32), 'encoder_attention_mask': jnp.ones((B, LK), dtype=bool), 'ln1_w': jnp.ones((D,), jnp.float32), 'ln1_b': jnp.zeros((D,), jnp.float32), 'q_w': jax.random.normal(ks[2], (D, D), jnp.float32) * std, 'q_b': jnp.zeros((D,), jnp.float32), 'k_w': jax.random.normal(ks[3], (D, D), jnp.float32) * std, 'k_b': jnp.zeros((D,), jnp.float32), 'v_w': jax.random.normal(ks[4], (D, D), jnp.float32) * std, 'v_b': jnp.zeros((D,), jnp.float32), 'cproj_w': jax.random.normal(ks[5], (D, D), jnp.float32) * std, 'cproj_b': jnp.zeros((D,), jnp.float32), 'ln2_w': jnp.ones((D,), jnp.float32), 'ln2_b': jnp.zeros((D,), jnp.float32), 'fc_w': jax.random.normal(ks[6], (D, INNER), jnp.float32) * std, 'fc_b': jnp.zeros((INNER,), jnp.float32), 'proj_w': jax.random.normal(ks[7], (INNER, D), jnp.float32) * std, 'proj_b': jnp.zeros((D,), jnp.float32)}
        return inp
    _L0_xattn_all = _L0_xattn_setup()
    _L0_xattn_in = {k: v for k, v in _L0_xattn_all.items() if k in ('ln1_w', 'ln1_b', 'q_w', 'q_b', 'k_w', 'k_b', 'v_w', 'v_b', 'cproj_w', 'cproj_b', 'ln2_w', 'ln2_b', 'fc_w', 'fc_b', 'proj_w', 'proj_b')}
    del _L0_xattn_all

    def _L1_xattn_setup():
        import jax, jax.numpy as jnp
        import numpy as np
        B, P, K, H, NH = (4, 256, 32, 256, 16)
        DH = H // NH
        EPS = 1e-06

        def rmsnorm(x, w):
            var = jnp.mean(jnp.square(x), axis=-1, keepdims=True)
            return x * jax.lax.rsqrt(var + EPS) * w
        key = jax.random.key(seed)
        ks = jax.random.split(key, 12)
        s = 0.02
        return {'x': jax.random.normal(ks[0], (B, P, H), jnp.float32), 'latents': jax.random.normal(ks[1], (B, K, H), jnp.float32), 'attention_mask': jax.random.randint(ks[2], (B, P), 0, 2, jnp.int32), 'q_w': s * jax.random.normal(ks[3], (H, H), jnp.float32), 'q_b': jnp.zeros((H,), jnp.float32), 'kv_w': s * jax.random.normal(ks[4], (H, 2 * H), jnp.float32), 'kv_b': jnp.zeros((2 * H,), jnp.float32), 'out_w': s * jax.random.normal(ks[5], (H, H), jnp.float32), 'out_b': jnp.zeros((H,), jnp.float32), 'postnorm_w': jnp.ones((H,), jnp.float32), 'mlp_w1': s * jax.random.normal(ks[6], (H, 4 * H), jnp.float32), 'mlp_b1': jnp.zeros((4 * H,), jnp.float32), 'mlp_w2': s * jax.random.normal(ks[7], (4 * H, H), jnp.float32), 'mlp_b2': jnp.zeros((H,), jnp.float32)}
    _L1_xattn_all = _L1_xattn_setup()
    _L1_xattn_in = {k: v for k, v in _L1_xattn_all.items() if k in ('q_w', 'q_b', 'kv_w', 'kv_b', 'out_w', 'out_b', 'postnorm_w', 'mlp_w1', 'mlp_b1', 'mlp_w2', 'mlp_b2')}
    del _L1_xattn_all
    return {'x': x, 'ctx_2048': ctx_2048, 'mask_BxS2_bf1': mask_BxS2_bf1, 'mask_BxS2_ik0': mask_BxS2_ik0, 'L0_xattn_ln1_w': _L0_xattn_in['ln1_w'], 'L0_xattn_ln1_b': _L0_xattn_in['ln1_b'], 'L0_xattn_q_w': _L0_xattn_in['q_w'], 'L0_xattn_q_b': _L0_xattn_in['q_b'], 'L0_xattn_k_w': _L0_xattn_in['k_w'], 'L0_xattn_k_b': _L0_xattn_in['k_b'], 'L0_xattn_v_w': _L0_xattn_in['v_w'], 'L0_xattn_v_b': _L0_xattn_in['v_b'], 'L0_xattn_cproj_w': _L0_xattn_in['cproj_w'], 'L0_xattn_cproj_b': _L0_xattn_in['cproj_b'], 'L0_xattn_ln2_w': _L0_xattn_in['ln2_w'], 'L0_xattn_ln2_b': _L0_xattn_in['ln2_b'], 'L0_xattn_fc_w': _L0_xattn_in['fc_w'], 'L0_xattn_fc_b': _L0_xattn_in['fc_b'], 'L0_xattn_proj_w': _L0_xattn_in['proj_w'], 'L0_xattn_proj_b': _L0_xattn_in['proj_b'], 'L1_xattn_q_w': _L1_xattn_in['q_w'], 'L1_xattn_q_b': _L1_xattn_in['q_b'], 'L1_xattn_kv_w': _L1_xattn_in['kv_w'], 'L1_xattn_kv_b': _L1_xattn_in['kv_b'], 'L1_xattn_out_w': _L1_xattn_in['out_w'], 'L1_xattn_out_b': _L1_xattn_in['out_b'], 'L1_xattn_postnorm_w': _L1_xattn_in['postnorm_w'], 'L1_xattn_mlp_w1': _L1_xattn_in['mlp_w1'], 'L1_xattn_mlp_b1': _L1_xattn_in['mlp_b1'], 'L1_xattn_mlp_w2': _L1_xattn_in['mlp_w2'], 'L1_xattn_mlp_b2': _L1_xattn_in['mlp_b2']}

def reference(x, ctx_2048, mask_BxS2_bf1, mask_BxS2_ik0, L0_xattn_ln1_w, L0_xattn_ln1_b, L0_xattn_q_w, L0_xattn_q_b, L0_xattn_k_w, L0_xattn_k_b, L0_xattn_v_w, L0_xattn_v_b, L0_xattn_cproj_w, L0_xattn_cproj_b, L0_xattn_ln2_w, L0_xattn_ln2_b, L0_xattn_fc_w, L0_xattn_fc_b, L0_xattn_proj_w, L0_xattn_proj_b, L1_xattn_q_w, L1_xattn_q_b, L1_xattn_kv_w, L1_xattn_kv_b, L1_xattn_out_w, L1_xattn_out_b, L1_xattn_postnorm_w, L1_xattn_mlp_w1, L1_xattn_mlp_b1, L1_xattn_mlp_w2, L1_xattn_mlp_b2):
    import jax
    import jax.numpy as jnp

    def _L0_xattn_ref(hidden_states, encoder_hidden_states, encoder_attention_mask, ln1_w, ln1_b, q_w, q_b, k_w, k_b, v_w, v_b, cproj_w, cproj_b, ln2_w, ln2_b, fc_w, fc_b, proj_w, proj_b):
        import jax, jax.numpy as jnp
        import numpy as np
        D = 256
        H = 16
        HD = D // H
        INNER = 4 * D
        EPS = 1e-05

        def layer_norm(x, w, b):
            mu = jnp.mean(x, axis=-1, keepdims=True)
            var = jnp.mean(jnp.square(x - mu), axis=-1, keepdims=True)
            return (x - mu) * jax.lax.rsqrt(var + EPS) * w + b
        B, LQ, _ = hidden_states.shape
        LK = encoder_hidden_states.shape[1]
        residual = hidden_states
        x = layer_norm(hidden_states, ln1_w, ln1_b)
        q = (x @ q_w + q_b).reshape(B, LQ, H, HD).transpose(0, 2, 1, 3)
        k = (encoder_hidden_states @ k_w + k_b).reshape(B, LK, H, HD).transpose(0, 2, 1, 3)
        v = (encoder_hidden_states @ v_w + v_b).reshape(B, LK, H, HD).transpose(0, 2, 1, 3)
        scale = 1.0 / np.sqrt(HD).astype(np.float32)
        scores = jnp.einsum('bhqd,bhkd->bhqk', q, k) * scale
        mask = encoder_attention_mask[:, None, None, :]
        mask_value = jnp.finfo(scores.dtype).min
        scores = jnp.where(mask, scores, mask_value)
        attn = jax.nn.softmax(scores, axis=-1)
        out = jnp.einsum('bhqk,bhkd->bhqd', attn, v)
        out = out.transpose(0, 2, 1, 3).reshape(B, LQ, D)
        out = out @ cproj_w + cproj_b
        hidden = out + residual
        residual = hidden
        y = layer_norm(hidden, ln2_w, ln2_b)
        y = jax.nn.gelu(y @ fc_w + fc_b, approximate=True)
        y = y @ proj_w + proj_b
        return residual + y

    def _L1_xattn_ref(x, latents, attention_mask, q_w, q_b, kv_w, kv_b, out_w, out_b, postnorm_w, mlp_w1, mlp_b1, mlp_w2, mlp_b2):
        import jax, jax.numpy as jnp
        import numpy as np
        B, P, K, H, NH = (4, 256, 32, 256, 16)
        DH = H // NH
        EPS = 1e-06

        def rmsnorm(x, w):
            var = jnp.mean(jnp.square(x), axis=-1, keepdims=True)
            return x * jax.lax.rsqrt(var + EPS) * w
        b, p, _ = x.shape
        k_len = latents.shape[1]
        residual = latents
        h = jnp.concatenate([x, latents], axis=1)
        q = (latents @ q_w + q_b).reshape(b, k_len, NH, DH)
        kv = (h @ kv_w + kv_b).reshape(b, p + k_len, NH, DH, 2)
        kmat, v = (kv[..., 0], kv[..., 1])
        attn = jnp.einsum('bkhd,bnhd->bhkn', q, kmat) / DH
        full_mask = jnp.concatenate([attention_mask.astype(bool), jnp.ones((b, k_len), bool)], axis=-1)
        attn = jnp.where(full_mask[:, None, None, :], attn, -jnp.inf)
        attn = jax.nn.softmax(attn.astype(jnp.float32), axis=-1).astype(q.dtype)
        attn_out = jnp.einsum('bhkn,bnhd->bkhd', attn, v).reshape(b, k_len, H)
        attn_out = attn_out @ out_w + out_b + residual
        out = rmsnorm(attn_out, postnorm_w)
        out = jax.nn.gelu(out @ mlp_w1 + mlp_b1) @ mlp_w2 + mlp_b2
        return out + residual
    x = _L0_xattn_ref(x, ctx_2048, mask_BxS2_bf1, L0_xattn_ln1_w, L0_xattn_ln1_b, L0_xattn_q_w, L0_xattn_q_b, L0_xattn_k_w, L0_xattn_k_b, L0_xattn_v_w, L0_xattn_v_b, L0_xattn_cproj_w, L0_xattn_cproj_b, L0_xattn_ln2_w, L0_xattn_ln2_b, L0_xattn_fc_w, L0_xattn_fc_b, L0_xattn_proj_w, L0_xattn_proj_b)
    x = _L1_xattn_ref(ctx_2048, x, mask_BxS2_ik0, L1_xattn_q_w, L1_xattn_q_b, L1_xattn_kv_w, L1_xattn_kv_b, L1_xattn_out_w, L1_xattn_out_b, L1_xattn_postnorm_w, L1_xattn_mlp_w1, L1_xattn_mlp_b1, L1_xattn_mlp_w2, L1_xattn_mlp_b2)
    return x

_drawn_inputs = setup_inputs


def setup_inputs(seed=0):
    import zlib

    import numpy as np

    out = dict(_drawn_inputs(seed))
    spreads = {'L0_xattn_ln1_w': (1.0, 0.6),
     'L0_xattn_ln1_b': (0.0, 0.8),
     'L0_xattn_q_b': (0.0, 0.8),
     'L0_xattn_k_b': (0.0, 0.8),
     'L0_xattn_v_b': (0.0, 0.1),
     'L0_xattn_cproj_b': (0.0, 0.1),
     'L0_xattn_ln2_w': (1.0, 0.6),
     'L0_xattn_ln2_b': (0.0, 0.742),
     'L0_xattn_fc_b': (0.0, 0.1),
     'L0_xattn_proj_b': (0.0, 0.1),
     'L1_xattn_q_b': (0.0, 0.8),
     'L1_xattn_kv_b': (0.0, 0.8),
     'L1_xattn_out_b': (0.0, 0.8),
     'L1_xattn_postnorm_w': (1.0, 0.6),
     'L1_xattn_mlp_b1': (0.0, 0.1),
     'L1_xattn_mlp_b2': (0.0, 0.1)}
    factors = {'L0_xattn_q_w': 8.0,
     'L0_xattn_k_w': 8.0,
     'L1_xattn_q_w': 8.0,
     'L1_xattn_kv_w': 8.0,
     'L1_xattn_out_w': 8.0}
    for name, (base, spread) in spreads.items():
        noise = np.random.default_rng([zlib.crc32(name.encode()), seed]).standard_normal(out[name].shape)
        drawn = base * np.exp(spread * noise) if base else spread * noise
        out[name] = jnp.asarray(drawn.astype(out[name].dtype))
    for name, factor in factors.items():
        out[name] = (out[name] * factor).astype(out[name].dtype)
    return out
```

```python
from contextlib import ExitStack

import concourse.bass as bass
from concourse import mybir

F32 = mybir.dt.float32
F32R = mybir.dt.float32r
ALU = mybir.AluOpType
ACT = mybir.ActivationFunctionType
AX = mybir.AxisListType

P = 128
B = 8
D = 256
C = D // P
H = 16
HD = D // H
PAIRS = B // 2
T = 2 * P
JOBS = 2 * PAIRS
SLICES = 4
QUADS = H // 4
MASK_ROW, MAX_ROW = 96, 97
BIG = float(2.0 ** 100)
EPS = (1e-5, 1e-6)
SCALE = (0.25, 1.0 / 16.0)

RING = 6
W_RING = 5
PT_RING = 4

WQ, WK, WV, WO = range(4)
W_FC, W_PROJ = 8, 12
CHUNK_SLOT = [0, 1, 2, 3, 8, 12, 9, 13, 10, 14, 11, 15, 4, 5, 6, 7, 8, 12, 9, 13, 10, 14, 11, 15]
FIRST_L1, FIRST_L1_MLP = 12, 16

V_INW, V_INB, V_QB, V_KB, V_VB, V_NW, V_NB, V_FCB = 0, 2, 4, 6, 8, 10, 12, 14
V_LAYER = 22
V_PARITY = 2 * V_LAYER
V_COLS = V_PARITY + 2


def layer(j):
    return j // PAIRS


def sources(j):
    return 1 + layer(j)


def k_bursts_before(j):
    return sum(sources(i) for i in range(j))


def score_bursts(j, b):
    n = QUADS * sources(j)
    return [("S", j, b, i) for i in range(n)]


def burst_order():
    order = [("TI", 0), ("Q", 0), ("K", 0, 0), ("V", 0, 0)]
    order += score_bursts(0, 0)
    for j in range(JOBS + 1):
        if j > 0:
            order += [("H1", j - 1, i) for i in range(SLICES)]
        if j < JOBS:
            if j > 0:
                order += score_bursts(j, 0)
            order += score_bursts(j, 1)
            order += [("TM", j, 0), ("TM", j, 1)]
            if j + 1 < JOBS:
                order += [("TI", j + 1), ("Q", j + 1), ("K", j + 1, 0)]
            order += [("ST", j, 0, i) for i in range(QUADS * sources(j))]
            if j + 1 < JOBS and sources(j + 1) == 2:
                order += [("K", j + 1, 1)]
            order += [("ST", j, 1, i) for i in range(QUADS * sources(j))]
            order += [("TO", j, 0), ("TO", j, 1)]
            if j + 1 < JOBS:
                order += [("V", j + 1, 0)]
            order += [("TOT", j)]
            if j + 1 < JOBS and sources(j + 1) == 2:
                order += [("V", j + 1, 1)]
            order += [("OUT", j), ("TY", j)]
    return order


def xattn_kernel(nc, x, ctxT, weights, vectors, rows, ident, mask1, mask2, out):
    number = {name: n for n, name in enumerate(burst_order())}
    exp_number = {}
    for j in range(JOBS):
        for b in range(2):
            for i in range(QUADS * sources(j)):
                exp_number[j, b, i] = len(exp_number)

    with ExitStack() as ctx:
        def sb(name, shape, dt=F32):
            return ctx.enter_context(nc.sbuf_tensor(name, shape, dt))

        def sem(name):
            return ctx.enter_context(nc.semaphore(name))

        x_sb = sb("x_sb", [P, B, D])
        ctx_raw = sb("ctx_raw", [P, C, T])
        ctx_hi = sb("ctx_hi", [P, C, T], F32R)
        ctx_lo = sb("ctx_lo", [P, C, T], F32R)
        h_res_norm = sb("h_res_norm", [P, 2, D])
        yT = sb("yT", [P, C, T])
        spread_in = sb("spread_in", [P, 2])
        x_norm = sb("x_norm", [P, 2, D])
        inT = sb("inT", [P, C, T])
        in_hi = sb("in_hi", [P, C, T], F32R)
        in_lo = sb("in_lo", [P, C, T], F32R)
        q_raw = sb("q_raw", [P, C, T])
        q_hi = sb("q_hi", [P, 2, C, T], F32R)
        q_lo = sb("q_lo", [P, 2, C, T], F32R)
        k_hi = sb("k_hi", [P, 2, C, T], F32R)
        k_lo = sb("k_lo", [P, 2, C, T], F32R)
        q_stack = sb("q_stack", [P, 4, 2, C, T], F32R)
        k_stack = sb("k_stack", [P, 4, 2, C, T], F32R)
        v_ones = sb("v_ones", [P, 2, 2, H, 32])
        probs = sb("probs", [P, PT_RING, 4 * P])
        neg_max = sb("neg_max", [P, 2, H])
        neg_maxT = sb("neg_maxT", [H, 2, P], F32R)
        o_raw = sb("o_raw", [P, 2, QUADS * P])
        o_recip = sb("o_recip", [P, 2, H])
        o_norm = sb("o_norm", [P, 2, D])
        oT_hi = sb("oT_hi", [P, C, T], F32R)
        oT_lo = sb("oT_lo", [P, C, T], F32R)
        h_res = sb("h_res", [P, 2, D])
        y_hi = sb("y_hi", [P, C, T], F32R)
        y_lo = sb("y_lo", [P, C, T], F32R)
        gelu_raw = sb("gelu_raw", [P, 2, 2, T])
        hid_hi = sb("hid_hi", [P, 2, 2, T], F32R)
        hid_lo = sb("hid_lo", [P, 2, 2, T], F32R)
        w_raw = sb("w_raw", [P, W_RING, 2 * D])
        w_hi = sb("w_hi", [P, 16, 2, D], F32R)
        w_lo = sb("w_lo", [P, 16, 2, D], F32R)
        vec = sb("vec", [P, V_COLS])
        bias_rows = sb("bias_rows", [P, 4, D])
        ident_sb = sb("ident_sb", [P, P])
        stats_in = sb("stats_in", [P, 2, 6])
        moments_in = sb("moments_in", [P, 2, 2])
        rstd_in = sb("rstd_in", [P, 2])
        stats = sb("stats", [P, 2, 6])
        moments = sb("moments", [P, 2, 2])
        spread = sb("spread", [P, 2])
        rstd = sb("rstd", [P, 2])
        minus_half = sb("minus_half", [P, 2])
        mask1_all = sb("mask1_all", [P, B, P], mybir.dt.uint8)
        mask1_sb = sb("mask1_sb", [B, P], mybir.dt.uint8)
        mask2_sb = sb("mask2_sb", [B, P], mybir.dt.int32)
        mask_any = sb("mask_any", [B, 1])
        mask_tmp = sb("mask_tmp", [B, P])
        mask_bias = sb("mask_bias", [B, 3, P], F32R)
        scale0 = sb("scale0", [P, B])

        banks = [ctx.enter_context(nc.psum_tensor(f"bank{i}", [P, 512], F32)) for i in range(RING)]
        o_bank = ctx.enter_context(nc.psum_tensor("o_bank", [P, 512], F32))
        mlp_bank = ctx.enter_context(nc.psum_tensor("mlp_bank", [P, 512], F32))

        bank_full = [sem(f"bank_full{i}") for i in range(RING)]
        bank_drained = [sem(f"bank_drained{i}") for i in range(RING)]
        o_full, o_drained = sem("o_full"), sem("o_drained")
        mlp_full, mlp_drained = sem("mlp_full"), sem("mlp_drained")
        x_in = [sem(f"x_in{g}") for g in range(PAIRS)]
        ctx_in, consts_in, masks_in = sem("ctx_in"), sem("consts_in"), sem("masks_in")
        w_in = [sem(f"w_in{i}") for i in range(W_RING)]
        w_hi_done, w_lo_dve, w_lo_pool = sem("w_hi_done"), sem("w_lo_dve"), sem("w_lo_pool")
        consts_set, ones_set, masks_set = sem("consts_set"), sem("ones_set"), sem("masks_set")
        ctx_hi_done, ctx_split = sem("ctx_hi_done"), sem("ctx_split")
        x_moments, x_rstd, x_normed = sem("x_moments"), sem("x_rstd"), sem("x_normed")
        in_steps, in_split = sem("in_steps"), sem("in_split")
        q_raw_done, q_split = sem("q_raw_done"), sem("q_split")
        k_hi_done, k_lo_half = sem("k_hi_done"), sem("k_lo_half")
        q_stacked, k_stacked = sem("q_stacked"), sem("k_stacked")
        max_stacked = [sem(f"max_stacked{b}") for b in range(2)]
        max_turned = sem("max_turned")
        probs_used = sem("probs_used")
        recip_done = sem("recip_done")
        oT_hi_done, oT_lo_half = sem("oT_hi_done"), sem("oT_lo_half")
        res_base, out_base = sem("res_base"), sem("out_base")
        ln_steps, rstd_done, h_normed = sem("ln_steps"), sem("rstd_done"), sem("h_normed")
        y_steps, y_split = sem("y_steps"), sem("y_split")
        gelu_done, hid_hi_done, hid_split, hid_used = sem("gelu_done"), sem("hid_hi_done"), sem("hid_split"), sem("hid_used")
        stored = sem("stored")
        pool_half = sem("pool_half")
        dve_step = sem("dve_step")

        def wait_full(eng, *name):
            n = number[name]
            eng.wait_ge(bank_full[n % RING], n // RING + 1)
            return banks[n % RING]

        def wait_drained(eng, *name):
            n = number[name]
            eng.wait_ge(bank_drained[n % RING], n // RING + 1)

        def drained(*name):
            return bank_drained[number[name] % RING]

        def wait_probs_used(eng, m):
            for (j, b, i), k in exp_number.items():
                if k == m:
                    if i == QUADS * sources(j) - 1:
                        eng.wait_ge(o_full, 2 * j + b + 1)
                    else:
                        eng.wait_ge(probs_used, m + 1 - (2 * j + b))

        def wait_hid_used(eng, n):
            j, i = n // SLICES, n % SLICES
            if i == SLICES - 1:
                eng.wait_ge(mlp_full, j + 1)
            else:
                eng.wait_ge(hid_used, (SLICES - 1) * j + i + 1)

        def col(ell, first, c):
            k = ell * V_LAYER + first + c
            return vec[:, k:k + 1]

        LN_STEPS = 5

        block = ctx.enter_context(nc.Block())

        @block.sync
        def _(sp):
            def load_weights(first, last):
                for n in range(first, last):
                    if n >= W_RING:
                        m = n - W_RING
                        if m < FIRST_L1:
                            sp.wait_ge(w_lo_dve, m + 1)
                        else:
                            sp.wait_ge(w_lo_pool, m + 1 - FIRST_L1)
                    sp.dma_start(w_raw[:, n % W_RING, :], weights[n]).then_inc(w_in[n % W_RING], 16)

            def load_ctx(j):
                if j > 0:
                    sp.wait_ge(ctx_split, j)
                sp.dma_start(ctx_raw[:], ctxT[j % PAIRS]).then_inc(ctx_in, 16)

            def load_x(g):
                sp.dma_start(x_sb[:, 2 * g:2 * g + 2, :], x[2 * g:2 * g + 2].rearrange("b p n -> p b n")).then_inc(x_in[g], 16)

            def stack(j):
                if j > 0:
                    sp.wait_ge(o_full, 2 * j)
                sp.wait_ge(q_split, 4 * (j + 1))
                for r, part in enumerate((q_hi, q_lo, q_hi)):
                    for p in range(4):
                        sp.dma_start(q_stack[32 * r:32 * r + 32, p].bitcast(F32),
                                     part[32 * p:32 * p + 32].bitcast(F32)).then_inc(q_stacked, 16)
                for s in range(sources(j)):
                    wait_drained(sp, "K", j, s)
                    for r, part in enumerate((k_hi, k_hi, k_lo)):
                        for p in range(4):
                            sp.dma_start(k_stack[32 * r:32 * r + 32, p, s].bitcast(F32),
                                         part[32 * p:32 * p + 32, s].bitcast(F32)).then_inc(k_stacked, 16)
                if j == 0:
                    sp.wait_ge(masks_set, 4)
                    sp.wait_ge(ones_set, 2)
                g = j % PAIRS
                for b in range(2):
                    for s in range(sources(j)):
                        which = 2 if s else layer(j)
                        src = mask_bias[2 * g + b:2 * g + b + 1, which, :].bitcast(F32)
                        for p in range(4):
                            sp.dma_start(k_stack[MASK_ROW:MASK_ROW + 1, p, s, :, b * P:b * P + P].bitcast(F32),
                                         src.rearrange("a (o n) -> a o n", o=1).to_broadcast([1, C, P])).then_inc(k_stacked, 16)

            def stack_max(j, b):
                wait_drained(sp, "TM", j, b)
                dst = q_stack[MAX_ROW:MAX_ROW + 1, :, :, :, b * P:b * P + P].bitcast(F32)
                sp.dma_start(dst.rearrange("o p e c n -> o (p e c) n"),
                             neg_maxT[:, b, :].bitcast(F32)).then_inc(max_stacked[b], 16)

            def store(g):
                sp.wait_ge(mlp_drained, PAIRS + g + 1)
                sp.dma_start(out[2 * g:2 * g + 2].rearrange("b p n -> p b n"), x_sb[:, 2 * g:2 * g + 2, :]).then_inc(stored, 16)

            load_x(0)
            sp.dma_start(vec[:], vectors).then_inc(consts_in, 16)
            sp.dma_start(ident_sb[:], ident).then_inc(consts_in, 16)
            load_ctx(0)
            load_weights(0, 3)
            sp.dma_start(mask1_sb[:], mask1).then_inc(masks_in, 16)
            sp.dma_start(mask2_sb[:], mask2).then_inc(masks_in, 16)
            sp.dma_start(mask1_all[:], mask1.rearrange("b n -> (b n)").partition_broadcast(P)).then_inc(masks_in, 16)
            sp.dma_start(bias_rows[:], rows.rearrange("r n -> (r n)").partition_broadcast(P)).then_inc(consts_in, 16)
            load_weights(3, W_RING)
            stack(0)
            load_weights(W_RING, FIRST_L1)
            for g in range(1, PAIRS):
                load_x(g)
            stack_max(0, 0)
            stack_max(0, 1)
            load_ctx(1)
            stack(1)
            for j in range(1, JOBS):
                if j == 1:
                    load_weights(FIRST_L1, FIRST_L1_MLP)
                if j == 2:
                    load_weights(FIRST_L1_MLP, FIRST_L1_MLP + W_RING)
                stack_max(j, 0)
                stack_max(j, 1)
                if j + 1 < JOBS:
                    load_ctx(j + 1)
                if j == 4:
                    load_weights(FIRST_L1_MLP + W_RING, len(CHUNK_SLOT))
                if j + 1 < JOBS:
                    stack(j + 1)
                if j > PAIRS:
                    store(j - PAIRS - 1)
            store(PAIRS - 1)
            sp.wait_ge(stored, 16 * PAIRS)

        @block.tensor
        def _(pe):
            opened = [0]

            def take_bank(*name):
                n = number[name]
                assert n == opened[0], (name, n, opened[0])
                opened[0] += 1
                if n >= RING:
                    pe.wait_ge(bank_drained[n % RING], n // RING)
                return banks[n % RING], bank_full[n % RING]

            def product(dst, a_hi, a_lo, b_hi, b_lo, first, last, shared=False):
                parts = [(a_hi, b_hi), (a_hi, b_lo), (a_lo, b_hi)]
                for k, (a, m) in enumerate(parts):
                    mm = pe.matmul(dst, a, m, start=first and k == 0, stop=last and k == 2, skip_group_check=shared)
                return mm

            def weight(slot, k, cols):
                return w_hi[:, slot, k, cols], w_lo[:, slot, k, cols]

            def wait_weights(upto):
                if upto <= FIRST_L1:
                    pe.wait_ge(w_lo_dve, upto)
                else:
                    pe.wait_ge(w_lo_pool, upto - FIRST_L1)

            def features(name, slot, hi, lo):
                bank, full = take_bank(*name)
                for m in range(C):
                    for k in range(C):
                        a = weight(slot, k, slice(m * P, m * P + P))
                        mm = product(bank[:, m * T:m * T + T], *a, hi[:, k, :], lo[:, k, :], k == 0, k == C - 1)
                mm.then_inc(full, 1)

            def tokens(name, slot, hi, lo):
                bank, full = take_bank(*name)
                for t in range(2):
                    for k in range(C):
                        cols = slice(t * P, t * P + P)
                        mm = product(bank[:, t * D:t * D + D], hi[:, k, cols], lo[:, k, cols],
                                     *weight(slot, k, slice(0, D)), k == 0, k == C - 1)
                mm.then_inc(full, 1)

            def turn_tokens(name, src):
                bank, full = take_bank(*name)
                for c in range(C):
                    for t in range(2):
                        mm = pe.transpose(bank[:, c * T + t * P:c * T + t * P + P], src[:, t, c * P:c * P + P], ident_sb[:])
                mm.then_inc(full, 1)

            def turn_inputs(j):
                if layer(j) == 0:
                    pe.wait_ge(x_normed, 2 * (j + 1))
                    turn_tokens(("TI", j), x_norm)
                else:
                    g = j % PAIRS
                    pe.wait_ge(mlp_drained, g + 1)
                    turn_tokens(("TI", j), x_sb[:, 2 * g:2 * g + 2, :])

            def queries(j):
                pe.wait_ge(in_split, j + 1)
                wait_weights((0 if layer(j) == 0 else FIRST_L1) + WQ + 1)
                features(("Q", j), 4 * layer(j) + WQ, in_hi, in_lo)

            def keys(j, s):
                if s == 0:
                    pe.wait_ge(ctx_split, j + 1)
                wait_weights((0 if layer(j) == 0 else FIRST_L1) + WK + 1)
                features(("K", j, s), 4 * layer(j) + WK, *((in_hi, in_lo) if s else (ctx_hi, ctx_lo)))

            def values(j, s):
                wait_weights((0 if layer(j) == 0 else FIRST_L1) + WV + 1)
                tokens(("V", j, s), 4 * layer(j) + WV, *((in_hi, in_lo) if s else (ctx_hi, ctx_lo)))

            def scores(j, b):
                n = sources(j)
                if b == 0:
                    pe.wait_ge(q_stacked, 16 * 12 * (j + 1))
                    pe.wait_ge(k_stacked, 16 * 20 * (k_bursts_before(j) + n))
                cols = slice(b * P, b * P + P)
                rows_ = slice(0, MASK_ROW + 1)
                for name in score_bursts(j, b):
                    bank, full = take_bank(*name)
                    i = name[3]
                    pairs = (2 * (i % 2), 2 * (i % 2) + 1) if n == 1 else (i % 4,)
                    c = i // 2 if n == 1 else i // 4
                    for k, p in enumerate(pairs):
                        for e in range(2):
                            at = (2 * k + e) * n * P
                            mm = pe.matmul(bank[:, at:at + n * P], q_stack[rows_, p, e, c, cols],
                                           k_stack[rows_, p, 0:n, c, cols], start=True, stop=True)
                    mm.then_inc(full, 1)

            def turn_max(j, b):
                wait_drained(pe, *score_bursts(j, b)[-1])
                bank, full = take_bank("TM", j, b)
                pe.transpose(bank[0:H, 0:P], neg_max[:, b, :], ident_sb[:]).then_inc(full, 1)

            def attend(j, b):
                n = sources(j)
                cols = slice(b * P, b * P + P)
                pe.wait_ge(max_stacked[b], 16 * (j + 1))

                def shifted(i):
                    quad, s = i // n, i % n
                    bank, full = take_bank("ST", j, b, i)
                    for k in range(2):
                        p = 2 * (quad % 2) + k
                        mm = pe.matmul(bank[:, k * T:k * T + T], k_stack[0:MAX_ROW + 1, p, s, quad // 2, cols],
                                       q_stack[0:MAX_ROW + 1, p, :, quad // 2, cols], start=True, stop=True)
                    mm.then_inc(full, 1)

                def weigh(i):
                    quad, s = i // n, i % n
                    wait_drained(pe, "ST", j, b, i)
                    if i == 0:
                        if b == 0:
                            wait_drained(pe, "V", j, n - 1)
                        if 2 * j + b > 0:
                            pe.wait_ge(o_drained, 2 * j + b)
                    slot = exp_number[j, b, i] % PT_RING
                    for h in range(4):
                        mm = pe.matmul(o_bank[32 * h:32 * h + 32, quad * P:quad * P + P],
                                       v_ones[:, b, s, 4 * quad + h, :], probs[:, slot, h * P:h * P + P],
                                       start=s == 0, stop=s == n - 1)
                    if i == QUADS * n - 1:
                        mm.then_inc(o_full, 1)
                    else:
                        mm.then_inc(probs_used, 1)

                last = QUADS * n
                for i in range(last + 2):
                    if i < last:
                        shifted(i)
                    if i >= 2:
                        weigh(i - 2)

            def turn_out(j, b):
                pe.wait_ge(o_drained, 2 * j + b + 1)
                bank, full = take_bank("TO", j, b)
                for i in range(QUADS):
                    mm = pe.transpose(bank[:, i * P:i * P + P], o_raw[:, b, i * P:i * P + P], ident_sb[:])
                mm.then_inc(full, 1)

            def turn_back(j):
                wait_drained(pe, "TO", j, 0)
                wait_drained(pe, "TO", j, 1)
                turn_tokens(("TOT", j), o_norm)

            def attention_out(j):
                wait_drained(pe, "TOT", j)
                if j == 0:
                    wait_weights(WO + 1)
                tokens(("OUT", j), 4 * layer(j) + WO, oT_hi, oT_lo)

            def turn_hidden(j):
                pe.wait_ge(h_normed, 2 * (j + 1))
                turn_tokens(("TY", j), h_res_norm)

            def mlp_up(j, i):
                if i == 0:
                    pe.wait_ge(y_split, j + 1)
                if j in (0, PAIRS):
                    wait_weights((4 if j == 0 else FIRST_L1_MLP) + 2 * i + 1)
                features(("H1", j, i), W_FC + i, y_hi, y_lo)

            def mlp_down(j, i):
                pe.wait_ge(hid_split, SLICES * j + i + 1)
                if i == 0 and j > 0:
                    pe.wait_ge(mlp_drained, j)
                if j in (0, PAIRS):
                    wait_weights((4 if j == 0 else FIRST_L1_MLP) + 2 * i + 2)
                for k in range(2):
                    for t in range(2):
                        a = (hid_hi[:, i % 2, k, t * P:t * P + P], hid_lo[:, i % 2, k, t * P:t * P + P])
                        mm = product(mlp_bank[:, t * D:t * D + D], *a, *weight(W_PROJ + i, k, slice(0, D)),
                                     i == 0 and k == 0 and t == 0, i == SLICES - 1 and k == 1, shared=True)
                mm.then_inc(mlp_full if i == SLICES - 1 else hid_used, 1)

            pe.wait_ge(consts_in, 48)
            turn_inputs(0)
            queries(0)
            keys(0, 0)
            values(0, 0)
            scores(0, 0)
            for j in range(JOBS + 1):
                more = j + 1 < JOBS
                if j > 0:
                    mlp_up(j - 1, 0)
                    mlp_up(j - 1, 1)
                    mlp_down(j - 1, 0)
                    mlp_up(j - 1, 2)
                    mlp_down(j - 1, 1)
                    mlp_up(j - 1, 3)
                    mlp_down(j - 1, 2)
                    mlp_down(j - 1, 3)
                if j < JOBS:
                    if j > 0:
                        scores(j, 0)
                    scores(j, 1)
                    turn_max(j, 0)
                    turn_max(j, 1)
                    if more:
                        turn_inputs(j + 1)
                        queries(j + 1)
                        keys(j + 1, 0)
                    attend(j, 0)
                    if more and sources(j + 1) == 2:
                        keys(j + 1, 1)
                    attend(j, 1)
                    turn_out(j, 0)
                    turn_out(j, 1)
                    if more:
                        values(j + 1, 0)
                    turn_back(j)
                    if more and sources(j + 1) == 2:
                        values(j + 1, 1)
                    attention_out(j)
                    turn_hidden(j)

        @block.scalar
        def _(act):
            def weights_hi(first, last):
                for n in range(first, last):
                    act.wait_ge(w_in[n % W_RING], 16 * (n // W_RING + 1))
                    if n == FIRST_L1_MLP:
                        act.wait_ge(mlp_full, PAIRS)
                    nc.scalar.activation(w_hi[:, CHUNK_SLOT[n]].rearrange("p a b -> p (a b)"), w_raw[:, n % W_RING, :],
                                         ACT.Copy).then_inc(w_hi_done, 1)

            def ctx_parts(j):
                act.wait_ge(ctx_in, 16 * (j + 1))
                if j > 0:
                    wait_full(act, "V", j - 1, 0)
                nc.scalar.activation(ctx_hi[:], ctx_raw[:], ACT.Copy).then_inc(ctx_hi_done, 1)

            def query_bias(j):
                bank = wait_full(act, "Q", j)
                if j > 0:
                    act.wait_ge(q_split, 4 * j)
                for c in range(C):
                    nc.scalar.activation(q_raw[:, c, :], bank[:, c * T:c * T + T], ACT.Identity,
                                         bias=col(layer(j), V_QB, c)).then_inc(drained("Q", j) if c == C - 1 else q_raw_done, 1)

            def key_hi(j, s):
                bank = wait_full(act, "K", j, s)
                if j > 0:
                    act.wait_ge(k_stacked, 16 * 20 * k_bursts_before(j))
                for c in range(C):
                    nc.scalar.activation(k_hi[:, s, c, :], bank[:, c * T:c * T + T], ACT.Identity,
                                         bias=col(layer(j), V_KB, c)).then_inc(k_hi_done, 1)

            def value_copy(j, s):
                bank = wait_full(act, "V", j, s)
                if j == 0:
                    act.wait_ge(ones_set, 4)
                else:
                    act.wait_ge(o_full, 2 * j)
                nc.scalar.activation(v_ones[:, :, s, :, 0:HD], bank[:].rearrange("p (t h d) -> p t h d", t=2, h=H),
                                     ACT.Copy).then_inc(drained("V", j, s), 1)

            def exponentials(j, b):
                n = sources(j)
                for i in range(QUADS * n):
                    bank = wait_full(act, "ST", j, b, i)
                    m = exp_number[j, b, i]
                    if m >= PT_RING:
                        wait_probs_used(act, m - PT_RING)
                    if layer(j) == 0:
                        batch = 2 * (j % PAIRS) + b
                        scale = scale0[:, batch:batch + 1]
                    else:
                        scale = SCALE[1]
                    nc.scalar.activation(probs[:, m % PT_RING, :], bank[:], ACT.Exp, scale=scale).then_inc(drained("ST", j, b, i), 1)

            def out_hi(j):
                bank = wait_full(act, "TOT", j)
                for c in range(C):
                    nc.scalar.activation(oT_hi[:, c, :], bank[:, c * T:c * T + T], ACT.Identity,
                                         bias=col(layer(j), V_VB, c)).then_inc(oT_hi_done, 1)

            def gelu(j, i):
                bank = wait_full(act, "H1", j, i)
                n = SLICES * j + i
                if n >= 2:
                    act.wait_ge(hid_split, n - 1)
                for f in range(2):
                    nc.scalar.activation(gelu_raw[:, i % 2, f, :], bank[:, f * T:f * T + T], ACT.Gelu_apprx_tanh,
                                         bias=col(layer(j), V_FCB, 2 * i + f)).then_inc(drained("H1", j, i) if f else gelu_done, 1)

            act.wait_ge(consts_in, 48)
            ctx_parts(0)
            weights_hi(0, 3)
            query_bias(0)
            key_hi(0, 0)
            value_copy(0, 0)
            act.wait_ge(masks_set, 5)
            weights_hi(3, FIRST_L1)
            for j in range(JOBS + 1):
                more = j + 1 < JOBS
                if j > 0:
                    for i in range(SLICES):
                        gelu(j - 1, i)
                if j < JOBS:
                    if j == 1:
                        weights_hi(FIRST_L1, FIRST_L1_MLP)
                    if more:
                        ctx_parts(j + 1)
                        query_bias(j + 1)
                        key_hi(j + 1, 0)
                    exponentials(j, 0)
                    if more and sources(j + 1) == 2:
                        key_hi(j + 1, 1)
                    exponentials(j, 1)
                    if more:
                        value_copy(j + 1, 0)
                    out_hi(j)
                    if more and sources(j + 1) == 2:
                        value_copy(j + 1, 1)
                    if j == PAIRS:
                        weights_hi(FIRST_L1_MLP, len(CHUNK_SLOT))

        @block.vector
        def _(dve):
            steps = [0]

            def link(ins):
                steps[0] += 1
                ins.then_inc(dve_step, 1)
                dve.wait_ge(dve_step, steps[0])

            def setup_masks():
                dve.wait_ge(masks_in, 48)
                nc.vector.tensor_reduce(mask_any[:], mask1_sb[:], AX.X, ALU.max).then_inc(masks_set, 1)
                nc.vector.tensor_scalar(mask_tmp[:], mask1_sb[:], -1.0, BIG, ALU.add, ALU.mult).then_inc(masks_set, 1)
                dve.wait_ge(masks_set, 2)
                nc.vector.tensor_scalar(mask_bias[:, 0, :], mask_tmp[:], mask_any[:], None, ALU.mult).then_inc(masks_set, 1)
                nc.vector.tensor_scalar(mask_bias[:, 1, :], mask2_sb[:], 0.0, -BIG, ALU.is_equal, ALU.mult).then_inc(masks_set, 1)
                link(nc.vector.tensor_reduce(scale0[:], mask1_all[:], AX.X, ALU.max))
                nc.vector.tensor_scalar(scale0[:], scale0[:], SCALE[0], None, ALU.mult).then_inc(masks_set, 1)

            def weights_lo(first, last):
                for n in range(first, last):
                    dve.wait_ge(w_hi_done, n + 1)
                    s = CHUNK_SLOT[n]
                    nc.vector.tensor_tensor(w_lo[:, s].rearrange("p a b -> p (a b)"), w_raw[:, n % W_RING, :],
                                            w_hi[:, s].rearrange("p a b -> p (a b)").bitcast(F32), ALU.subtract).then_inc(w_lo_dve, 1)

            def input_norm(j):
                g = j % PAIRS
                dve.wait_ge(x_in[g], 16)
                for t in range(2):
                    nc.vector.bn_stats(stats_in[:, t, :], x_sb[:, 2 * g + t, :]).then_inc(x_moments, 1)
                dve.wait_ge(x_moments, 6 * j + 2)
                if j > 0:
                    dve.wait_ge(x_normed, 2 * j)
                for t in range(2):
                    nc.vector.bn_aggr(moments_in[:, t, :], stats_in[:, t, :]).then_inc(x_moments, 1)
                dve.wait_ge(x_moments, 6 * j + 4)
                if j > 0:
                    dve.wait_ge(x_rstd, j)
                for t in range(2):
                    nc.vector.tensor_scalar(spread_in[:, t:t + 1], moments_in[:, t, 1:2], EPS[0], None, ALU.add).then_inc(x_moments, 1)

            def input_norm_apply(j):
                g = j % PAIRS
                dve.wait_ge(x_rstd, j + 1)
                if j > 0:
                    wait_full(dve, "TI", j - 1)
                for t in range(2):
                    nc.vector.tensor_scalar(x_norm[:, t, :], x_sb[:, 2 * g + t, :], moments_in[:, t, 0:1], rstd_in[:, t:t + 1],
                                            ALU.subtract, ALU.mult).then_inc(x_normed, 1)

            def ctx_parts(j):
                dve.wait_ge(ctx_hi_done, j + 1)
                nc.vector.tensor_tensor(ctx_lo[:], ctx_raw[:], ctx_hi[:].bitcast(F32), ALU.subtract).then_inc(ctx_split, 1)

            def input_parts(j):
                bank = wait_full(dve, "TI", j)
                for c in range(C):
                    src = bank[:, c * T:c * T + T]
                    if layer(j) == 0:
                        ins = nc.vector.tensor_scalar(inT[:, c, :], src, col(0, V_INW, c), col(0, V_INB, c), ALU.mult, ALU.add)
                    else:
                        ins = nc.vector.tensor_copy(inT[:, c, :], src)
                    ins.then_inc(drained("TI", j) if c == C - 1 else in_steps, 1)
                wait_drained(dve, "TI", j)
                if j > 0:
                    wait_full(dve, "V", j - 1, sources(j - 1) - 1)
                nc.vector.tensor_copy(in_hi[:], inT[:]).then_inc(in_steps, 1)
                dve.wait_ge(in_steps, 2 * (j + 1))
                nc.vector.tensor_tensor(in_lo[:], inT[:], in_hi[:].bitcast(F32), ALU.subtract).then_inc(in_split, 1)

            def query_parts(j):
                wait_drained(dve, "Q", j)
                if j > 0:
                    dve.wait_ge(q_stacked, 16 * 12 * j)
                for e in range(2):
                    nc.vector.tensor_scalar(q_hi[:, e], q_raw[:], vec[:, V_PARITY + e:V_PARITY + e + 1], None, ALU.mult).then_inc(q_split, 1)
                dve.wait_ge(q_split, 4 * j + 2)
                for e in range(2):
                    nc.vector.scalar_tensor_tensor(q_lo[:, e], q_raw[:], vec[:, V_PARITY + e:V_PARITY + e + 1],
                                                   q_hi[:, e].bitcast(F32), ALU.mult, ALU.subtract).then_inc(q_split, 1)

            def key_lo(j, s):
                bank = wait_full(dve, "K", j, s)
                dve.wait_ge(k_hi_done, C * (k_bursts_before(j) + s + 1))
                for c in range(C):
                    ins = nc.vector.scalar_tensor_tensor(k_lo[:, s, c, :], bank[:, c * T:c * T + T], col(layer(j), V_KB, c),
                                                         k_hi[:, s, c, :].bitcast(F32), ALU.add, ALU.subtract)
                    ins.then_inc(drained("K", j, s) if c == C - 1 else k_lo_half, 1)

            def maxima(j, b):
                n = sources(j)
                for name in score_bursts(j, b):
                    bank = wait_full(dve, *name)
                    heads = 4 // n
                    i = name[3]
                    if i == 0 and j > 0:
                        wait_full(dve, "TM", j - 1, b)
                    first = 8 * (i % 2) + i // 2 if n == 1 else 4 * (i % 4) + i // 4
                    nc.vector.tensor_reduce(neg_max[:, b, first:first + 2 * heads - 1:2],
                                            bank[:].rearrange("p (h n) -> p h n", h=heads), AX.X, ALU.max,
                                            negate=True).then_inc(drained(*name), 1)

            def max_rows(j, b):
                bank = wait_full(dve, "TM", j, b)
                if j > 0:
                    dve.wait_ge(max_stacked[b], 16 * j)
                nc.vector.tensor_copy(neg_maxT[:, b, :], bank[0:H, 0:P]).then_inc(drained("TM", j, b), 1)

            def take_heads(j, b):
                dve.wait_ge(o_full, 2 * j + b + 1)
                if j > 0:
                    wait_full(dve, "TO", j - 1, b)
                nc.vector.tensor_copy(o_raw[:, b, :], o_bank[:]).then_inc(o_drained, 1)

            def normalise_heads(j, b):
                bank = wait_full(dve, "TO", j, b)
                by_head = bank[:].rearrange("p (h w) -> p h w", w=32)
                u = 2 * j + b
                if j > 0:
                    wait_full(dve, "TOT", j - 1)
                nc.vector.reciprocal(o_recip[:, b, :].rearrange("p (h o) -> p h o", o=1), by_head[:, :, HD:HD + 1]).then_inc(recip_done, 1)
                dve.wait_ge(recip_done, u + 1)
                nc.vector.tensor_tensor(o_norm[:, b, :].rearrange("p (h d) -> p h d", d=HD), by_head[:, :, 0:HD],
                                        o_recip[:, b, :].rearrange("p (h o) -> p h o", o=1).to_broadcast([P, H, HD]),
                                        ALU.mult).then_inc(drained("TO", j, b), 1)

            def out_lo(j):
                bank = wait_full(dve, "TOT", j)
                dve.wait_ge(oT_hi_done, C * (j + 1))
                for c in range(C):
                    ins = nc.vector.scalar_tensor_tensor(oT_lo[:, c, :], bank[:, c * T:c * T + T], col(layer(j), V_VB, c),
                                                         oT_hi[:, c, :].bitcast(F32), ALU.add, ALU.subtract)
                    ins.then_inc(drained("TOT", j) if c == C - 1 else oT_lo_half, 1)

            def residual(j):
                bank = wait_full(dve, "OUT", j)
                dve.wait_ge(res_base, j + 1)
                nc.vector.tensor_tensor(h_res[:].rearrange("p t n -> p (t n)"), bank[:], h_res[:].rearrange("p t n -> p (t n)"),
                                        ALU.add).then_inc(drained("OUT", j), 1)

            def hidden_norm(j):
                ell = layer(j)
                wait_drained(dve, "OUT", j)
                for t in range(2):
                    link(nc.vector.bn_stats(stats[:, t, :], h_res[:, t, :]))
                for t in range(2):
                    link(nc.vector.bn_aggr(moments[:, t, :], stats[:, t, :]))
                if ell == 0:
                    nc.vector.tensor_scalar(spread[:], moments[:, :, 1], EPS[0], None, ALU.add).then_inc(ln_steps, 1)
                else:
                    link(nc.vector.tensor_tensor(spread[:], moments[:, :, 0], moments[:, :, 0], ALU.mult))
                    link(nc.vector.tensor_tensor(spread[:], spread[:], moments[:, :, 1], ALU.add))
                    nc.vector.tensor_scalar(spread[:], spread[:], EPS[1], None, ALU.add).then_inc(ln_steps, 1)
                dve.wait_ge(rstd_done, j + 1)
                for t in range(2):
                    if ell == 0:
                        ins = nc.vector.tensor_scalar(h_res_norm[:, t, :], h_res[:, t, :], moments[:, t, 0:1], rstd[:, t:t + 1],
                                                      ALU.subtract, ALU.mult)
                    else:
                        ins = nc.vector.tensor_scalar(h_res_norm[:, t, :], h_res[:, t, :], rstd[:, t:t + 1], None, ALU.mult)
                    ins.then_inc(h_normed, 1)

            def hidden_parts(j):
                bank = wait_full(dve, "TY", j)
                for c in range(C):
                    nc.vector.tensor_scalar(yT[:, c, :], bank[:, c * T:c * T + T], col(layer(j), V_NW, c), col(layer(j), V_NB, c),
                                            ALU.mult, ALU.add).then_inc(drained("TY", j) if c == C - 1 else y_steps, 1)
                wait_drained(dve, "TY", j)
                nc.vector.tensor_copy(y_hi[:], yT[:]).then_inc(y_steps, 1)
                dve.wait_ge(y_steps, 2 * (j + 1))
                nc.vector.tensor_tensor(y_lo[:], yT[:], y_hi[:].bitcast(F32), ALU.subtract).then_inc(y_split, 1)

            def gelu_hi(j, i):
                wait_drained(dve, "H1", j, i)
                n = SLICES * j + i
                if n >= 2:
                    wait_hid_used(dve, n - 2)
                nc.vector.tensor_copy(hid_hi[:, i % 2], gelu_raw[:, i % 2]).then_inc(hid_hi_done, 1)

            def finish(j):
                g = j % PAIRS
                dve.wait_ge(mlp_full, j + 1)
                dve.wait_ge(out_base, j + 1)
                xg = x_sb[:, 2 * g:2 * g + 2, :].rearrange("p t n -> p (t n)")
                nc.vector.tensor_tensor(xg, mlp_bank[:], xg, ALU.add).then_inc(mlp_drained, 1)

            dve.wait_ge(consts_in, 48)
            input_norm(0)
            input_norm_apply(0)
            ctx_parts(0)
            weights_lo(0, 1)
            input_parts(0)
            weights_lo(1, 3)
            query_parts(0)
            key_lo(0, 0)
            setup_masks()
            maxima(0, 0)
            weights_lo(3, FIRST_L1)
            for j in range(JOBS + 1):
                more = j + 1 < JOBS
                if j > 0:
                    for i in range(SLICES):
                        gelu_hi(j - 1, i)
                if j < JOBS:
                    if more and layer(j + 1) == 0:
                        input_norm(j + 1)
                    if j > 0:
                        finish(j - 1)
                        maxima(j, 0)
                    maxima(j, 1)
                    max_rows(j, 0)
                    max_rows(j, 1)
                    if more:
                        if layer(j + 1) == 0:
                            input_norm_apply(j + 1)
                        ctx_parts(j + 1)
                        input_parts(j + 1)
                        query_parts(j + 1)
                        key_lo(j + 1, 0)
                    take_heads(j, 0)
                    if more and sources(j + 1) == 2:
                        key_lo(j + 1, 1)
                    take_heads(j, 1)
                    normalise_heads(j, 0)
                    normalise_heads(j, 1)
                    out_lo(j)
                    residual(j)
                    hidden_norm(j)
                    hidden_parts(j)
                else:
                    finish(j - 1)

        @block.gpsimd
        def _(pool):
            nc.gpsimd.memset(minus_half[:], -0.5).then_inc(consts_set, 1)
            pool.wait_ge(consts_set, 1)
            nc.gpsimd.memset(mask_bias[:, 2, :].bitcast(F32), 0.0).then_inc(consts_set, 1)
            pool.wait_ge(consts_set, 2)
            nc.gpsimd.memset(k_stack[MASK_ROW:MASK_ROW + 2].bitcast(F32), 1.0).then_inc(ones_set, 1)
            pool.wait_ge(ones_set, 1)
            nc.gpsimd.memset(q_stack[MASK_ROW:MASK_ROW + 2].bitcast(F32), 1.0).then_inc(ones_set, 1)
            pool.wait_ge(ones_set, 2)
            nc.gpsimd.memset(v_ones[:], 0.0).then_inc(ones_set, 1)
            pool.wait_ge(ones_set, 3)
            nc.gpsimd.memset(v_ones[:, :, :, :, HD:HD + 1], 1.0).then_inc(ones_set, 1)
            pool.wait_ge(ones_set, 4)

            def input_rstd(j):
                pool.wait_ge(x_moments, 6 * (j + 1))
                nc.gpsimd.tensor_tensor(rstd_in[:], spread_in[:], minus_half[:], ALU.pow).then_inc(x_rstd, 1)

            def residual_base(j):
                g = j % PAIRS
                if layer(j) == 1:
                    pool.wait_ge(mlp_drained, g + 1)
                else:
                    pool.wait_ge(x_in[g], 16)
                for t in range(2):
                    ins = nc.gpsimd.tensor_tensor(h_res[:, t, :], x_sb[:, 2 * g + t, :], bias_rows[:, 2 * layer(j), :], ALU.add)
                    ins.then_inc(res_base if t else pool_half, 1)

            def hidden_rstd(j):
                pool.wait_ge(ln_steps, j + 1)
                nc.gpsimd.tensor_tensor(rstd[:], spread[:], minus_half[:], ALU.pow).then_inc(rstd_done, 1)

            def output_base(j):
                g = j % PAIRS
                wait_drained(pool, "OUT", j)
                if layer(j) == 1:
                    pool.wait_ge(res_base, j + 1)
                for t in range(2):
                    src = h_res[:, t, :] if layer(j) == 0 else x_sb[:, 2 * g + t, :]
                    ins = nc.gpsimd.tensor_tensor(x_sb[:, 2 * g + t, :], src, bias_rows[:, 2 * layer(j) + 1, :], ALU.add)
                    ins.then_inc(out_base if t else pool_half, 1)

            def weights_lo(first, last):
                for n in range(first, last):
                    pool.wait_ge(w_hi_done, n + 1)
                    s = CHUNK_SLOT[n]
                    nc.gpsimd.tensor_tensor(w_lo[:, s].rearrange("p a b -> p (a b)"), w_raw[:, n % W_RING, :],
                                            w_hi[:, s].rearrange("p a b -> p (a b)").bitcast(F32), ALU.subtract).then_inc(w_lo_pool, 1)

            def gelu_lo(j, i):
                pool.wait_ge(hid_hi_done, SLICES * j + i + 1)
                nc.gpsimd.tensor_tensor(hid_lo[:, i % 2], gelu_raw[:, i % 2], hid_hi[:, i % 2].bitcast(F32),
                                        ALU.subtract).then_inc(hid_split, 1)

            input_rstd(0)
            pool.wait_ge(consts_in, 48)
            residual_base(0)
            for j in range(JOBS + 1):
                if j > 0:
                    for i in range(SLICES):
                        gelu_lo(j - 1, i)
                if j < JOBS:
                    if j + 1 < PAIRS:
                        input_rstd(j + 1)
                    if j == 1:
                        weights_lo(FIRST_L1, FIRST_L1_MLP)
                    if j > 0:
                        residual_base(j)
                    hidden_rstd(j)
                    output_base(j)
                    if j == PAIRS:
                        weights_lo(FIRST_L1_MLP, len(CHUNK_SLOT))


def kernel(**inputs):
    import numpy as np
    import concourse.bacc as bacc
    from concourse.bass_utils import run_bass_kernel_spmd

    a = {k: np.asarray(v) for k, v in inputs.items()}
    l0 = lambda n: a["L0_xattn_" + n]
    l1 = lambda n: a["L1_xattn_" + n]

    def square(w):
        return w.reshape(C, P, D).transpose(1, 0, 2).reshape(1, P, C * D)

    def wide(w):
        return w.reshape(C, P, SLICES, D).transpose(2, 1, 0, 3).reshape(SLICES, P, C * D)

    def tall(w):
        return w.reshape(SLICES, 2, P, D).transpose(0, 2, 1, 3).reshape(SLICES, P, 2 * D)

    def mlp(up, down):
        return np.stack([wide(up), tall(down)], axis=1).reshape(2 * SLICES, P, 2 * D)

    kv = l1("kv_w").reshape(D, D, 2)
    weights = np.concatenate([square(l0("q_w")), square(l0("k_w")), square(l0("v_w")), square(l0("cproj_w")),
                              mlp(l0("fc_w"), l0("proj_w")),
                              square(l1("q_w")), square(kv[:, :, 0]), square(kv[:, :, 1]), square(l1("out_w")),
                              mlp(l1("mlp_w1"), l1("mlp_w2"))])

    def cols(v):
        return v.reshape(-1, P).T

    kvb = l1("kv_b").reshape(D, 2)
    zero, one = np.zeros(D, np.float32), np.ones(D, np.float32)
    head = (np.arange(P) // HD) % 2
    parity = np.stack([head == 0, head == 1], axis=1).astype(np.float32)
    vectors = np.concatenate(
        [cols(v) for v in (l0("ln1_w"), l0("ln1_b"), l0("q_b"), l0("k_b"), l0("v_b"), l0("ln2_w"), l0("ln2_b"), l0("fc_b"))]
        + [cols(v) for v in (one, zero, l1("q_b"), kvb[:, 0], kvb[:, 1], l1("postnorm_w"), zero, l1("mlp_b1"))]
        + [parity], axis=1)
    arrays = {
        "x": a["x"],
        "ctxT": a["ctx_2048"].reshape(PAIRS, T, C, P).transpose(0, 3, 2, 1),
        "weights": weights,
        "vectors": vectors,
        "rows": np.stack([l0("cproj_b"), l0("proj_b"), l1("out_b"), l1("mlp_b2")]),
        "ident": np.eye(P, dtype=np.float32),
        "mask1": a["mask_BxS2_bf1"].view(np.uint8),
        "mask2": a["mask_BxS2_ik0"],
    }
    arrays = {k: np.ascontiguousarray(v) for k, v in arrays.items()}
    nc = bacc.Bacc("TRN2", target_bir_lowering=False, num_devices=1)
    args = [nc.dram_tensor(k, v.shape, mybir.dt.from_np(v.dtype), kind="ExternalInput").ap() for k, v in arrays.items()]
    args.append(nc.dram_tensor("out", (B, P, D), F32, kind="ExternalOutput").ap())
    xattn_kernel(nc, *args)
    r = run_bass_kernel_spmd(nc, [arrays], core_ids=[0])
    return r.results[0]["out"]
```

```python
from contextlib import ExitStack

import concourse.bass as bass
from concourse import mybir

F32 = mybir.dt.float32
F32R = mybir.dt.float32r
ALU = mybir.AluOpType
ACT = mybir.ActivationFunctionType
AX = mybir.AxisListType

P = 128
B = 8
D = 256
C = D // P
H = 16
HD = D // H
PAIRS = B // 2
T = 2 * P
JOBS = 2 * PAIRS
SLICES = 4
QUADS = H // 4
MASK_ROW, MAX_ROW = 96, 97
BIG = float(2.0 ** 100)
EPS = (1e-5, 1e-6)
SCALE = (0.25, 1.0 / 16.0)

RING = 6
W_RING = 8
PT_RING = 4

WQ, WK, WV, WO = range(4)
W_FC, W_PROJ = 8, 12
CHUNK_SLOT = [0, 1, 2, 3, 8, 12, 9, 13, 10, 14, 11, 15, 4, 5, 6, 7, 8, 12, 9, 13, 10, 14, 11, 15]
FIRST_L1, FIRST_L1_MLP = 12, 16

V_INW, V_INB, V_QB, V_KB, V_VB, V_NW, V_NB, V_FCB = 0, 2, 4, 6, 8, 10, 12, 14
V_LAYER = 22
V_PARITY = 2 * V_LAYER
V_COLS = V_PARITY + 2


def layer(j):
    return j // PAIRS


def sources(j):
    return 1 + layer(j)


def k_bursts_before(j):
    return sum(sources(i) for i in range(j))


def k_stacked_by(j):
    return 16 * (12 * k_bursts_before(j) + 2 * j)


def score_bursts(j, b):
    n = QUADS * sources(j)
    return [("S", j, b, i) for i in range(n)]


def burst_order():
    order = [("TI", 0), ("Q", 0), ("K", 0, 0), ("V", 0, 0), ("TI", 1)]
    order += score_bursts(0, 0) + score_bursts(0, 1)
    for j in range(JOBS):
        more, two = j + 1 < JOBS, j + 1 < JOBS and sources(j + 1) == 2
        order += [("TM", j, 0)]
        order += [("Q", j + 1)] if more else []
        order += [("TM", j, 1)]
        order += [("K", j + 1, 0)] if more else []
        order += [("K", j + 1, 1)] if two else []
        order += [("ST", j, b, i) for b in range(2) for i in range(QUADS * sources(j))]
        order += [("TO", j, 0)]
        order += [("H1", j - 1, 0)] if j > 0 else []
        order += [("TO", j, 1)]
        order += [("H1", j - 1, 1)] if j > 0 else []
        order += [("V", j + 1, 0)] if more else []
        order += [("TOT", j)]
        order += [("H1", j - 1, 2)] if j > 0 else []
        order += [("V", j + 1, 1)] if two else []
        order += [("OUT", j)]
        order += [("H1", j - 1, 3)] if j > 0 else []
        order += [("TY", j)]
        order += [("TI", j + 2)] if j + 2 < JOBS else []
        order += score_bursts(j + 1, 0) + score_bursts(j + 1, 1) if more else []
    order += [("H1", JOBS - 1, i) for i in range(SLICES)]
    return order


def xattn_kernel(nc, x, ctxT, weights, vectors, rows, ident, mask1, mask2, out):
    number = {name: n for n, name in enumerate(burst_order())}
    exp_number = {}
    for j in range(JOBS):
        for b in range(2):
            for i in range(QUADS * sources(j)):
                exp_number[j, b, i] = len(exp_number)

    with ExitStack() as ctx:
        def sb(name, shape, dt=F32):
            return ctx.enter_context(nc.sbuf_tensor(name, shape, dt))

        def sem(name):
            return ctx.enter_context(nc.semaphore(name))

        x_sb = sb("x_sb", [P, B, D])
        ctx_raw = sb("ctx_raw", [P, C, T])
        ctx_hi = sb("ctx_hi", [P, C, T], F32R)
        ctx_lo = sb("ctx_lo", [P, C, T], F32R)
        h_res_norm = sb("h_res_norm", [P, 2, D])
        spread_in = sb("spread_in", [P, 2])
        x_norm = sb("x_norm", [P, 2, D])
        turned = sb("turned", [P, C, T])
        in_hi = sb("in_hi", [P, C, T], F32R)
        in_lo = sb("in_lo", [P, C, T], F32R)
        q_raw = sb("q_raw", [P, C, T])
        q_hi = sb("q_hi", [P, 2, C, T], F32R)
        q_lo = sb("q_lo", [P, 2, C, T], F32R)
        k_hi = sb("k_hi", [P, 2, C, T], F32R)
        k_lo = sb("k_lo", [P, 2, C, T], F32R)
        q_stack = sb("q_stack", [P, 4, 2, C, T], F32R)
        k_stack = sb("k_stack", [P, 2, 4, C, T], F32R)
        v_ones = sb("v_ones", [P, 2, 2, H, 32])
        probs = sb("probs", [P, PT_RING, 4 * P])
        neg_max = sb("neg_max", [P, 2, H])
        neg_maxT = sb("neg_maxT", [H, 2, P], F32R)
        o_raw = sb("o_raw", [P, 2, QUADS * P])
        o_recip = sb("o_recip", [P, 2, H])
        o_norm = sb("o_norm", [P, 2, D])
        oT_hi = sb("oT_hi", [P, C, T], F32R)
        oT_lo = sb("oT_lo", [P, C, T], F32R)
        h_res = sb("h_res", [P, 2, D])
        y_hi = sb("y_hi", [P, C, T], F32R)
        y_lo = sb("y_lo", [P, C, T], F32R)
        gelu_raw = sb("gelu_raw", [P, 2, 2, T])
        hid_hi = sb("hid_hi", [P, 2, 2, T], F32R)
        hid_lo = sb("hid_lo", [P, 2, 2, T], F32R)
        w_raw = sb("w_raw", [P, W_RING, 2 * D])
        w_hi = sb("w_hi", [P, 16, 2, D], F32R)
        w_lo = sb("w_lo", [P, 16, 2, D], F32R)
        vec = sb("vec", [P, V_COLS])
        bias_rows = sb("bias_rows", [P, 4, D])
        ident_sb = sb("ident_sb", [P, P])
        stats_in = sb("stats_in", [P, 2, 6])
        moments_in = sb("moments_in", [P, 2, 2])
        rstd_in = sb("rstd_in", [P, 2])
        stats = sb("stats", [P, 2, 6])
        moments = sb("moments", [P, 2, 2])
        spread = sb("spread", [P, 2])
        rstd = sb("rstd", [P, 2])
        minus_half = sb("minus_half", [P, 2])
        mask1_all = sb("mask1_all", [P, B, P], mybir.dt.uint8)
        mask1_sb = sb("mask1_sb", [B, P], mybir.dt.uint8)
        mask2_sb = sb("mask2_sb", [B, P], mybir.dt.int32)
        mask_any = sb("mask_any", [B, 1])
        mask_tmp = sb("mask_tmp", [B, P])
        mask_bias = sb("mask_bias", [B, 2, P], F32R)
        scale0 = sb("scale0", [P, B])

        banks = [ctx.enter_context(nc.psum_tensor(f"bank{i}", [P, 512], F32)) for i in range(RING)]
        o_bank = ctx.enter_context(nc.psum_tensor("o_bank", [P, 512], F32))
        mlp_bank = ctx.enter_context(nc.psum_tensor("mlp_bank", [P, 512], F32))

        bank_full = [sem(f"bank_full{i}") for i in range(RING)]
        bank_drained = [sem(f"bank_drained{i}") for i in range(RING)]
        o_full, o_drained = sem("o_full"), sem("o_drained")
        mlp_full, mlp_drained = sem("mlp_full"), sem("mlp_drained")
        x_in = [sem(f"x_in{g}") for g in range(PAIRS)]
        ctx_in, consts_in, masks_in = sem("ctx_in"), sem("consts_in"), sem("masks_in")
        w_in = [sem(f"w_in{i}") for i in range(W_RING)]
        w_hi_done, w_lo_dve, w_lo_pool = sem("w_hi_done"), sem("w_lo_dve"), sem("w_lo_pool")
        consts_set, ones_set, masks_set = sem("consts_set"), sem("ones_set"), sem("masks_set")
        ctx_hi_done, ctx_split = sem("ctx_hi_done"), sem("ctx_split")
        x_moments, x_rstd, x_normed = sem("x_moments"), sem("x_rstd"), sem("x_normed")
        in_steps, in_split = sem("in_steps"), sem("in_split")
        q_raw_done, q_split = sem("q_raw_done"), sem("q_split")
        k_hi_done, k_lo_half = sem("k_hi_done"), sem("k_lo_half")
        q_stacked, k_stacked = sem("q_stacked"), sem("k_stacked")
        max_stacked = [sem(f"max_stacked{b}") for b in range(2)]
        max_turned = sem("max_turned")
        probs_used = sem("probs_used")
        recip_done = sem("recip_done")
        oT_hi_done, oT_lo_half = sem("oT_hi_done"), sem("oT_lo_half")
        res_base, out_base = sem("res_base"), sem("out_base")
        ln_steps, rstd_done, h_normed = sem("ln_steps"), sem("rstd_done"), sem("h_normed")
        y_steps, y_split = sem("y_steps"), sem("y_split")
        gelu_done, hid_hi_done, hid_split, hid_used = sem("gelu_done"), sem("hid_hi_done"), sem("hid_split"), sem("hid_used")
        stored = sem("stored")
        pool_half = sem("pool_half")
        dve_step = sem("dve_step")

        def wait_full(eng, *name):
            n = number[name]
            eng.wait_ge(bank_full[n % RING], n // RING + 1)
            return banks[n % RING]

        def wait_drained(eng, *name):
            n = number[name]
            eng.wait_ge(bank_drained[n % RING], n // RING + 1)

        def drained(*name):
            return bank_drained[number[name] % RING]

        def wait_probs_used(eng, m):
            for (j, b, i), k in exp_number.items():
                if k == m:
                    if i == QUADS * sources(j) - 1:
                        eng.wait_ge(o_full, 2 * j + b + 1)
                    else:
                        eng.wait_ge(probs_used, m + 1 - (2 * j + b))

        def wait_hid_used(eng, n):
            j, i = n // SLICES, n % SLICES
            if i == SLICES - 1:
                eng.wait_ge(mlp_full, j + 1)
            else:
                eng.wait_ge(hid_used, (SLICES - 1) * j + i + 1)

        def col(ell, first, c):
            k = ell * V_LAYER + first + c
            return vec[:, k:k + 1]

        LN_STEPS = 5

        block = ctx.enter_context(nc.Block())

        @block.sync
        def _(sp):
            def load_weights(first, last):
                for n in range(first, last):
                    if n >= W_RING:
                        m = n - W_RING
                        if m < FIRST_L1:
                            sp.wait_ge(w_lo_dve, m + 1)
                        else:
                            sp.wait_ge(w_lo_pool, m + 1 - FIRST_L1)
                    sp.dma_start(w_raw[:, n % W_RING, :], weights[n]).then_inc(w_in[n % W_RING], 16)

            def load_ctx(j):
                if j > 0:
                    sp.wait_ge(ctx_split, j)
                sp.dma_start(ctx_raw[:], ctxT[j % PAIRS]).then_inc(ctx_in, 16)

            def load_x(g):
                sp.dma_start(x_sb[:, 2 * g:2 * g + 2, :], x[2 * g:2 * g + 2].rearrange("b p n -> p b n")).then_inc(x_in[g], 16)

            def stack(j):
                if j > 0:
                    sp.wait_ge(o_full, 2 * j)
                sp.wait_ge(q_split, 4 * (j + 1))
                for r, part in enumerate((q_hi, q_lo, q_hi)):
                    for p in range(4):
                        sp.dma_start(q_stack[32 * r:32 * r + 32, p].bitcast(F32),
                                     part[32 * p:32 * p + 32].bitcast(F32)).then_inc(q_stacked, 16)
                for s in range(sources(j)):
                    wait_drained(sp, "K", j, s)
                    for r, part in enumerate((k_hi, k_hi, k_lo)):
                        for p in range(4):
                            sp.dma_start(k_stack[32 * r:32 * r + 32, s, p].bitcast(F32),
                                         part[32 * p:32 * p + 32, s].bitcast(F32)).then_inc(k_stacked, 16)
                if j == 0:
                    sp.wait_ge(masks_set, 4)
                    sp.wait_ge(ones_set, 2)
                g = j % PAIRS
                for b in range(2):
                    dst = k_stack[MASK_ROW:MASK_ROW + 1, 0, :, :, b * P:b * P + P].rearrange("o p c n -> o (p c) n")
                    src = mask_bias[2 * g + b:2 * g + b + 1, layer(j):layer(j) + 1, :].bitcast(F32)
                    sp.dma_start(dst.bitcast(F32), src.to_broadcast([1, 4 * C, P])).then_inc(k_stacked, 16)

            def stack_max(j, b):
                wait_drained(sp, "TM", j, b)
                dst = q_stack[MAX_ROW:MAX_ROW + 1, :, :, :, b * P:b * P + P].bitcast(F32)
                sp.dma_start(dst.rearrange("o p e c n -> o (p e c) n"),
                             neg_maxT[:, b, :].bitcast(F32)).then_inc(max_stacked[b], 16)

            def store(g):
                sp.wait_ge(mlp_drained, PAIRS + g + 1)
                sp.dma_start(out[2 * g:2 * g + 2].rearrange("b p n -> p b n"), x_sb[:, 2 * g:2 * g + 2, :]).then_inc(stored, 16)

            load_x(0)
            sp.dma_start(vec[:], vectors).then_inc(consts_in, 16)
            sp.dma_start(ident_sb[:], ident).then_inc(consts_in, 16)
            load_ctx(0)
            load_weights(0, 3)
            sp.dma_start(mask1_sb[:], mask1).then_inc(masks_in, 16)
            sp.dma_start(mask2_sb[:], mask2).then_inc(masks_in, 16)
            sp.dma_start(mask1_all[:], mask1.rearrange("b n -> (b n)").partition_broadcast(P)).then_inc(masks_in, 16)
            sp.dma_start(bias_rows[:], rows.rearrange("r n -> (r n)").partition_broadcast(P)).then_inc(consts_in, 16)
            load_x(1)
            load_ctx(1)
            load_weights(3, 5)
            stack(0)
            load_weights(5, 5 + W_RING - 2)
            load_x(2)
            load_x(3)
            for j in range(JOBS):
                if j + 2 < JOBS:
                    load_ctx(j + 2)
                stack_max(j, 0)
                stack_max(j, 1)
                if j + 1 < JOBS:
                    stack(j + 1)
                if j == 0:
                    load_weights(5 + W_RING - 2, FIRST_L1)
                if j == 1:
                    load_weights(FIRST_L1, FIRST_L1_MLP)
                if j == 2:
                    load_weights(FIRST_L1_MLP, len(CHUNK_SLOT))
                if j > PAIRS:
                    store(j - PAIRS - 1)
            store(PAIRS - 1)
            sp.wait_ge(stored, 16 * PAIRS)

        @block.tensor
        def _(pe):
            opened = [0]

            def take_bank(*name):
                n = number[name]
                assert n == opened[0], (name, n, opened[0])
                opened[0] += 1
                if n >= RING:
                    pe.wait_ge(bank_drained[n % RING], n // RING)
                return banks[n % RING], bank_full[n % RING]

            def product(dst, a_hi, a_lo, b_hi, b_lo, first, last, shared=False):
                parts = [(a_hi, b_hi), (a_hi, b_lo), (a_lo, b_hi)]
                for k, (a, m) in enumerate(parts):
                    mm = pe.matmul(dst, a, m, start=first and k == 0, stop=last and k == 2, skip_group_check=shared)
                return mm

            def weight(slot, k, cols):
                return w_hi[:, slot, k, cols], w_lo[:, slot, k, cols]

            def wait_weights(upto):
                if upto <= FIRST_L1:
                    pe.wait_ge(w_lo_dve, upto)
                else:
                    pe.wait_ge(w_lo_pool, upto - FIRST_L1)

            def features(name, slot, hi, lo):
                bank, full = take_bank(*name)
                for m in range(C):
                    for k in range(C):
                        a = weight(slot, k, slice(m * P, m * P + P))
                        mm = product(bank[:, m * T:m * T + T], *a, hi[:, k, :], lo[:, k, :], k == 0, k == C - 1)
                mm.then_inc(full, 1)

            def tokens(name, slot, hi, lo):
                bank, full = take_bank(*name)
                for t in range(2):
                    for k in range(C):
                        cols = slice(t * P, t * P + P)
                        mm = product(bank[:, t * D:t * D + D], hi[:, k, cols], lo[:, k, cols],
                                     *weight(slot, k, slice(0, D)), k == 0, k == C - 1)
                mm.then_inc(full, 1)

            def turn_tokens(name, src):
                bank, full = take_bank(*name)
                for c in range(C):
                    for t in range(2):
                        mm = pe.transpose(bank[:, c * T + t * P:c * T + t * P + P], src[:, t, c * P:c * P + P], ident_sb[:])
                mm.then_inc(full, 1)

            def turn_inputs(j):
                if layer(j) == 0:
                    pe.wait_ge(x_normed, 2 * (j + 1))
                    turn_tokens(("TI", j), x_norm)
                else:
                    g = j % PAIRS
                    pe.wait_ge(mlp_drained, g + 1)
                    turn_tokens(("TI", j), x_sb[:, 2 * g:2 * g + 2, :])

            def queries(j):
                pe.wait_ge(in_split, j + 1)
                wait_weights((0 if layer(j) == 0 else FIRST_L1) + WQ + 1)
                features(("Q", j), 4 * layer(j) + WQ, in_hi, in_lo)

            def keys(j, s):
                if s == 0:
                    pe.wait_ge(ctx_split, j + 1)
                wait_weights((0 if layer(j) == 0 else FIRST_L1) + WK + 1)
                features(("K", j, s), 4 * layer(j) + WK, *((in_hi, in_lo) if s else (ctx_hi, ctx_lo)))

            def values(j, s):
                wait_weights((0 if layer(j) == 0 else FIRST_L1) + WV + 1)
                tokens(("V", j, s), 4 * layer(j) + WV, *((in_hi, in_lo) if s else (ctx_hi, ctx_lo)))

            def scores(j, b):
                n = sources(j)
                if b == 0:
                    pe.wait_ge(q_stacked, 16 * 12 * (j + 1))
                    pe.wait_ge(k_stacked, k_stacked_by(j + 1))
                cols = slice(b * P, b * P + P)
                rows_ = slice(0, MASK_ROW + 1)
                for name in score_bursts(j, b):
                    bank, full = take_bank(*name)
                    i = name[3]
                    pairs = (2 * (i % 2), 2 * (i % 2) + 1) if n == 1 else (i % 4,)
                    c = i // 2 if n == 1 else i // 4
                    for k, p in enumerate(pairs):
                        for e in range(2):
                            at = (2 * k + e) * n * P
                            mm = pe.matmul(bank[:, at:at + n * P], q_stack[rows_, p, e, c, cols],
                                           k_stack[rows_, 0:n, p, c, cols], start=True, stop=True)
                    mm.then_inc(full, 1)

            def turn_max(j, b):
                wait_drained(pe, *score_bursts(j, b)[-1])
                bank, full = take_bank("TM", j, b)
                pe.transpose(bank[0:H, 0:P], neg_max[:, b, :], ident_sb[:]).then_inc(full, 1)

            def attend(j, b):
                n = sources(j)
                cols = slice(b * P, b * P + P)
                pe.wait_ge(max_stacked[b], 16 * (j + 1))

                def shifted(i):
                    quad, s = i // n, i % n
                    bank, full = take_bank("ST", j, b, i)
                    for k in range(2):
                        p = 2 * (quad % 2) + k
                        mm = pe.matmul(bank[:, k * T:k * T + T], k_stack[0:MAX_ROW + 1, s, p, quad // 2, cols],
                                       q_stack[0:MAX_ROW + 1, p, :, quad // 2, cols], start=True, stop=True)
                    mm.then_inc(full, 1)

                def weigh(i):
                    quad, s = i // n, i % n
                    wait_drained(pe, "ST", j, b, i)
                    if i == 0:
                        if b == 0:
                            wait_drained(pe, "V", j, n - 1)
                        if 2 * j + b > 0:
                            pe.wait_ge(o_drained, 2 * j + b)
                    slot = exp_number[j, b, i] % PT_RING
                    for h in range(4):
                        mm = pe.matmul(o_bank[32 * h:32 * h + 32, quad * P:quad * P + P],
                                       v_ones[:, b, s, 4 * quad + h, :], probs[:, slot, h * P:h * P + P],
                                       start=s == 0, stop=s == n - 1)
                    if i == QUADS * n - 1:
                        mm.then_inc(o_full, 1)
                    else:
                        mm.then_inc(probs_used, 1)

                last = QUADS * n
                for i in range(last + 2):
                    if i < last:
                        shifted(i)
                    if i >= 2:
                        weigh(i - 2)

            def turn_out(j, b):
                pe.wait_ge(o_drained, 2 * j + b + 1)
                bank, full = take_bank("TO", j, b)
                for i in range(QUADS):
                    mm = pe.transpose(bank[:, i * P:i * P + P], o_raw[:, b, i * P:i * P + P], ident_sb[:])
                mm.then_inc(full, 1)

            def turn_back(j):
                wait_drained(pe, "TO", j, 0)
                wait_drained(pe, "TO", j, 1)
                turn_tokens(("TOT", j), o_norm)

            def attention_out(j):
                wait_drained(pe, "TOT", j)
                if j == 0:
                    wait_weights(WO + 1)
                tokens(("OUT", j), 4 * layer(j) + WO, oT_hi, oT_lo)

            def turn_hidden(j):
                pe.wait_ge(h_normed, 2 * (j + 1))
                turn_tokens(("TY", j), h_res_norm)

            def mlp_up(j, i):
                if i == 0:
                    pe.wait_ge(y_split, j + 1)
                if j in (0, PAIRS):
                    wait_weights((4 if j == 0 else FIRST_L1_MLP) + 2 * i + 1)
                features(("H1", j, i), W_FC + i, y_hi, y_lo)

            def mlp_down(j, i):
                pe.wait_ge(hid_split, SLICES * j + i + 1)
                if i == 0 and j > 0:
                    pe.wait_ge(mlp_drained, j)
                if j in (0, PAIRS):
                    wait_weights((4 if j == 0 else FIRST_L1_MLP) + 2 * i + 2)
                for k in range(2):
                    for t in range(2):
                        a = (hid_hi[:, i % 2, k, t * P:t * P + P], hid_lo[:, i % 2, k, t * P:t * P + P])
                        mm = product(mlp_bank[:, t * D:t * D + D], *a, *weight(W_PROJ + i, k, slice(0, D)),
                                     i == 0 and k == 0 and t == 0, i == SLICES - 1 and k == 1, shared=True)
                mm.then_inc(mlp_full if i == SLICES - 1 else hid_used, 1)

            pe.wait_ge(consts_in, 48)
            turn_inputs(0)
            queries(0)
            keys(0, 0)
            values(0, 0)
            turn_inputs(1)
            scores(0, 0)
            scores(0, 1)
            for j in range(JOBS):
                more, two = j + 1 < JOBS, j + 1 < JOBS and sources(j + 1) == 2
                mlp = j > 0
                turn_max(j, 0)
                if more:
                    queries(j + 1)
                turn_max(j, 1)
                if more:
                    keys(j + 1, 0)
                if two:
                    keys(j + 1, 1)
                attend(j, 0)
                attend(j, 1)
                turn_out(j, 0)
                if mlp:
                    mlp_up(j - 1, 0)
                turn_out(j, 1)
                if mlp:
                    mlp_up(j - 1, 1)
                if more:
                    values(j + 1, 0)
                turn_back(j)
                if mlp:
                    mlp_down(j - 1, 0)
                    mlp_up(j - 1, 2)
                if two:
                    values(j + 1, 1)
                attention_out(j)
                if mlp:
                    mlp_down(j - 1, 1)
                    mlp_up(j - 1, 3)
                    mlp_down(j - 1, 2)
                turn_hidden(j)
                if mlp:
                    mlp_down(j - 1, 3)
                if j + 2 < JOBS:
                    turn_inputs(j + 2)
                if more:
                    scores(j + 1, 0)
                    scores(j + 1, 1)
            last = JOBS - 1
            mlp_up(last, 0)
            mlp_up(last, 1)
            mlp_down(last, 0)
            mlp_up(last, 2)
            mlp_down(last, 1)
            mlp_up(last, 3)
            mlp_down(last, 2)
            mlp_down(last, 3)

        @block.scalar
        def _(act):
            def weights_hi(first, last):
                for n in range(first, last):
                    act.wait_ge(w_in[n % W_RING], 16 * (n // W_RING + 1))
                    if n == FIRST_L1_MLP:
                        act.wait_ge(mlp_full, PAIRS)
                    nc.scalar.activation(w_hi[:, CHUNK_SLOT[n]].rearrange("p a b -> p (a b)"), w_raw[:, n % W_RING, :],
                                         ACT.Copy).then_inc(w_hi_done, 1)

            def ctx_parts(j):
                act.wait_ge(ctx_in, 16 * (j + 1))
                if j > 0:
                    wait_full(act, "V", j - 1, 0)
                nc.scalar.activation(ctx_hi[:], ctx_raw[:], ACT.Copy).then_inc(ctx_hi_done, 1)

            def query_bias(j):
                bank = wait_full(act, "Q", j)
                if j > 0:
                    act.wait_ge(q_split, 4 * j)
                for c in range(C):
                    nc.scalar.activation(q_raw[:, c, :], bank[:, c * T:c * T + T], ACT.Identity,
                                         bias=col(layer(j), V_QB, c)).then_inc(drained("Q", j) if c == C - 1 else q_raw_done, 1)

            def key_hi(j, s):
                bank = wait_full(act, "K", j, s)
                if j > 0:
                    act.wait_ge(k_stacked, k_stacked_by(j))
                for c in range(C):
                    nc.scalar.activation(k_hi[:, s, c, :], bank[:, c * T:c * T + T], ACT.Identity,
                                         bias=col(layer(j), V_KB, c)).then_inc(k_hi_done, 1)

            def value_copy(j, s):
                bank = wait_full(act, "V", j, s)
                if j == 0:
                    act.wait_ge(ones_set, 4)
                else:
                    act.wait_ge(o_full, 2 * j)
                nc.scalar.activation(v_ones[:, :, s, :, 0:HD], bank[:].rearrange("p (t h d) -> p t h d", t=2, h=H),
                                     ACT.Copy).then_inc(drained("V", j, s), 1)

            def exponentials(j, b):
                n = sources(j)
                for i in range(QUADS * n):
                    bank = wait_full(act, "ST", j, b, i)
                    m = exp_number[j, b, i]
                    if m >= PT_RING:
                        wait_probs_used(act, m - PT_RING)
                    if layer(j) == 0:
                        batch = 2 * (j % PAIRS) + b
                        scale = scale0[:, batch:batch + 1]
                    else:
                        scale = SCALE[1]
                    nc.scalar.activation(probs[:, m % PT_RING, :], bank[:], ACT.Exp, scale=scale).then_inc(drained("ST", j, b, i), 1)

            def out_hi(j):
                bank = wait_full(act, "TOT", j)
                for c in range(C):
                    nc.scalar.activation(oT_hi[:, c, :], bank[:, c * T:c * T + T], ACT.Identity,
                                         bias=col(layer(j), V_VB, c)).then_inc(oT_hi_done, 1)

            def gelu(j, i):
                bank = wait_full(act, "H1", j, i)
                n = SLICES * j + i
                if n >= 2:
                    act.wait_ge(hid_split, n - 1)
                for f in range(2):
                    nc.scalar.activation(gelu_raw[:, i % 2, f, :], bank[:, f * T:f * T + T], ACT.Gelu_apprx_tanh,
                                         bias=col(layer(j), V_FCB, 2 * i + f)).then_inc(drained("H1", j, i) if f else gelu_done, 1)

            act.wait_ge(consts_in, 48)
            ctx_parts(0)
            weights_hi(0, 3)
            query_bias(0)
            key_hi(0, 0)
            value_copy(0, 0)
            ctx_parts(1)
            weights_hi(3, 5)
            act.wait_ge(masks_set, 5)
            for j in range(JOBS):
                more, two = j + 1 < JOBS, j + 1 < JOBS and sources(j + 1) == 2
                mlp = j > 0
                if more:
                    query_bias(j + 1)
                    key_hi(j + 1, 0)
                if two:
                    key_hi(j + 1, 1)
                if j == 2:
                    weights_hi(FIRST_L1, FIRST_L1_MLP)
                exponentials(j, 0)
                exponentials(j, 1)
                if mlp:
                    gelu(j - 1, 0)
                    gelu(j - 1, 1)
                if more:
                    value_copy(j + 1, 0)
                out_hi(j)
                if mlp:
                    gelu(j - 1, 2)
                if two:
                    value_copy(j + 1, 1)
                if mlp:
                    gelu(j - 1, 3)
                if j + 2 < JOBS:
                    ctx_parts(j + 2)
                if j == 0:
                    weights_hi(5, FIRST_L1)
                if j == PAIRS:
                    weights_hi(FIRST_L1_MLP, len(CHUNK_SLOT))
            for i in range(SLICES):
                gelu(JOBS - 1, i)

        @block.vector
        def _(dve):
            steps = [0]

            def link(ins):
                steps[0] += 1
                ins.then_inc(dve_step, 1)
                dve.wait_ge(dve_step, steps[0])

            def setup_masks():
                dve.wait_ge(masks_in, 48)
                nc.vector.tensor_reduce(mask_any[:], mask1_sb[:], AX.X, ALU.max).then_inc(masks_set, 1)
                nc.vector.tensor_scalar(mask_tmp[:], mask1_sb[:], -1.0, BIG, ALU.add, ALU.mult).then_inc(masks_set, 1)
                dve.wait_ge(masks_set, 2)
                nc.vector.tensor_scalar(mask_bias[:, 0, :], mask_tmp[:], mask_any[:], None, ALU.mult).then_inc(masks_set, 1)
                nc.vector.tensor_scalar(mask_bias[:, 1, :], mask2_sb[:], 0.0, -BIG, ALU.is_equal, ALU.mult).then_inc(masks_set, 1)
                link(nc.vector.tensor_reduce(scale0[:], mask1_all[:], AX.X, ALU.max))
                nc.vector.tensor_scalar(scale0[:], scale0[:], SCALE[0], None, ALU.mult).then_inc(masks_set, 1)

            def weights_lo(first, last):
                for n in range(first, last):
                    dve.wait_ge(w_hi_done, n + 1)
                    s = CHUNK_SLOT[n]
                    nc.vector.tensor_tensor(w_lo[:, s].rearrange("p a b -> p (a b)"), w_raw[:, n % W_RING, :],
                                            w_hi[:, s].rearrange("p a b -> p (a b)").bitcast(F32), ALU.subtract).then_inc(w_lo_dve, 1)

            def input_norm(j):
                g = j % PAIRS
                dve.wait_ge(x_in[g], 16)
                for t in range(2):
                    nc.vector.bn_stats(stats_in[:, t, :], x_sb[:, 2 * g + t, :]).then_inc(x_moments, 1)
                dve.wait_ge(x_moments, 6 * j + 2)
                if j > 0:
                    dve.wait_ge(x_normed, 2 * j)
                for t in range(2):
                    nc.vector.bn_aggr(moments_in[:, t, :], stats_in[:, t, :]).then_inc(x_moments, 1)
                dve.wait_ge(x_moments, 6 * j + 4)
                if j > 0:
                    dve.wait_ge(x_rstd, j)
                for t in range(2):
                    nc.vector.tensor_scalar(spread_in[:, t:t + 1], moments_in[:, t, 1:2], EPS[0], None, ALU.add).then_inc(x_moments, 1)

            def input_norm_apply(j):
                g = j % PAIRS
                dve.wait_ge(x_rstd, j + 1)
                if j > 0:
                    wait_full(dve, "TI", j - 1)
                for t in range(2):
                    nc.vector.tensor_scalar(x_norm[:, t, :], x_sb[:, 2 * g + t, :], moments_in[:, t, 0:1], rstd_in[:, t:t + 1],
                                            ALU.subtract, ALU.mult).then_inc(x_normed, 1)

            def ctx_parts(j):
                dve.wait_ge(ctx_hi_done, j + 1)
                nc.vector.tensor_tensor(ctx_lo[:], ctx_raw[:], ctx_hi[:].bitcast(F32), ALU.subtract).then_inc(ctx_split, 1)

            def input_parts(j):
                bank = wait_full(dve, "TI", j)
                if j >= 2:
                    dve.wait_ge(y_split, j - 1)
                elif j == 1:
                    dve.wait_ge(in_split, 1)
                for c in range(C):
                    src = bank[:, c * T:c * T + T]
                    if layer(j) == 0:
                        ins = nc.vector.tensor_scalar(turned[:, c, :], src, col(0, V_INW, c), col(0, V_INB, c), ALU.mult, ALU.add)
                    else:
                        ins = nc.vector.tensor_copy(turned[:, c, :], src)
                    ins.then_inc(drained("TI", j) if c == C - 1 else in_steps, 1)
                wait_drained(dve, "TI", j)
                if j > 0:
                    wait_full(dve, "V", j - 1, sources(j - 1) - 1)
                nc.vector.tensor_copy(in_hi[:], turned[:]).then_inc(in_steps, 1)
                dve.wait_ge(in_steps, 2 * (j + 1))
                nc.vector.tensor_tensor(in_lo[:], turned[:], in_hi[:].bitcast(F32), ALU.subtract).then_inc(in_split, 1)

            def query_parts(j):
                wait_drained(dve, "Q", j)
                if j > 0:
                    dve.wait_ge(q_stacked, 16 * 12 * j)
                for e in range(2):
                    nc.vector.tensor_scalar(q_hi[:, e], q_raw[:], vec[:, V_PARITY + e:V_PARITY + e + 1], None, ALU.mult).then_inc(q_split, 1)
                dve.wait_ge(q_split, 4 * j + 2)
                for e in range(2):
                    nc.vector.scalar_tensor_tensor(q_lo[:, e], q_raw[:], vec[:, V_PARITY + e:V_PARITY + e + 1],
                                                   q_hi[:, e].bitcast(F32), ALU.mult, ALU.subtract).then_inc(q_split, 1)

            def key_lo(j, s):
                bank = wait_full(dve, "K", j, s)
                dve.wait_ge(k_hi_done, C * (k_bursts_before(j) + s + 1))
                for c in range(C):
                    ins = nc.vector.scalar_tensor_tensor(k_lo[:, s, c, :], bank[:, c * T:c * T + T], col(layer(j), V_KB, c),
                                                         k_hi[:, s, c, :].bitcast(F32), ALU.add, ALU.subtract)
                    ins.then_inc(drained("K", j, s) if c == C - 1 else k_lo_half, 1)

            def maxima(j, b):
                n = sources(j)
                for name in score_bursts(j, b):
                    bank = wait_full(dve, *name)
                    heads = 4 // n
                    i = name[3]
                    if i == 0 and j > 0:
                        wait_full(dve, "TM", j - 1, b)
                    first = 8 * (i % 2) + i // 2 if n == 1 else 4 * (i % 4) + i // 4
                    nc.vector.tensor_reduce(neg_max[:, b, first:first + 2 * heads - 1:2],
                                            bank[:].rearrange("p (h n) -> p h n", h=heads), AX.X, ALU.max,
                                            negate=True).then_inc(drained(*name), 1)

            def max_rows(j, b):
                bank = wait_full(dve, "TM", j, b)
                if j > 0:
                    dve.wait_ge(max_stacked[b], 16 * j)
                nc.vector.tensor_copy(neg_maxT[:, b, :], bank[0:H, 0:P]).then_inc(drained("TM", j, b), 1)

            def take_heads(j, b):
                dve.wait_ge(o_full, 2 * j + b + 1)
                if j > 0:
                    wait_full(dve, "TO", j - 1, b)
                nc.vector.tensor_copy(o_raw[:, b, :], o_bank[:]).then_inc(o_drained, 1)

            def normalise_heads(j, b):
                bank = wait_full(dve, "TO", j, b)
                by_head = bank[:].rearrange("p (h w) -> p h w", w=32)
                u = 2 * j + b
                if j > 0:
                    wait_full(dve, "TOT", j - 1)
                nc.vector.reciprocal(o_recip[:, b, :].rearrange("p (h o) -> p h o", o=1), by_head[:, :, HD:HD + 1]).then_inc(recip_done, 1)
                dve.wait_ge(recip_done, u + 1)
                nc.vector.tensor_tensor(o_norm[:, b, :].rearrange("p (h d) -> p h d", d=HD), by_head[:, :, 0:HD],
                                        o_recip[:, b, :].rearrange("p (h o) -> p h o", o=1).to_broadcast([P, H, HD]),
                                        ALU.mult).then_inc(drained("TO", j, b), 1)

            def out_lo(j):
                bank = wait_full(dve, "TOT", j)
                dve.wait_ge(oT_hi_done, C * (j + 1))
                for c in range(C):
                    ins = nc.vector.scalar_tensor_tensor(oT_lo[:, c, :], bank[:, c * T:c * T + T], col(layer(j), V_VB, c),
                                                         oT_hi[:, c, :].bitcast(F32), ALU.add, ALU.subtract)
                    ins.then_inc(drained("TOT", j) if c == C - 1 else oT_lo_half, 1)

            def residual(j):
                bank = wait_full(dve, "OUT", j)
                dve.wait_ge(res_base, j + 1)
                nc.vector.tensor_tensor(h_res[:].rearrange("p t n -> p (t n)"), bank[:], h_res[:].rearrange("p t n -> p (t n)"),
                                        ALU.add).then_inc(drained("OUT", j), 1)

            def hidden_moments(j):
                ell = layer(j)
                wait_drained(dve, "OUT", j)
                for t in range(2):
                    link(nc.vector.bn_stats(stats[:, t, :], h_res[:, t, :]))
                for t in range(2):
                    link(nc.vector.bn_aggr(moments[:, t, :], stats[:, t, :]))
                if ell == 0:
                    nc.vector.tensor_scalar(spread[:], moments[:, :, 1], EPS[0], None, ALU.add).then_inc(ln_steps, 1)
                else:
                    link(nc.vector.tensor_tensor(spread[:], moments[:, :, 0], moments[:, :, 0], ALU.mult))
                    link(nc.vector.tensor_tensor(spread[:], spread[:], moments[:, :, 1], ALU.add))
                    nc.vector.tensor_scalar(spread[:], spread[:], EPS[1], None, ALU.add).then_inc(ln_steps, 1)

            def hidden_norm(j):
                dve.wait_ge(rstd_done, j + 1)
                for t in range(2):
                    if layer(j) == 0:
                        ins = nc.vector.tensor_scalar(h_res_norm[:, t, :], h_res[:, t, :], moments[:, t, 0:1], rstd[:, t:t + 1],
                                                      ALU.subtract, ALU.mult)
                    else:
                        ins = nc.vector.tensor_scalar(h_res_norm[:, t, :], h_res[:, t, :], rstd[:, t:t + 1], None, ALU.mult)
                    ins.then_inc(h_normed, 1)

            def hidden_parts(j):
                bank = wait_full(dve, "TY", j)
                dve.wait_ge(in_split, min(j + 2, JOBS))
                for c in range(C):
                    nc.vector.tensor_scalar(turned[:, c, :], bank[:, c * T:c * T + T], col(layer(j), V_NW, c), col(layer(j), V_NB, c),
                                            ALU.mult, ALU.add).then_inc(drained("TY", j) if c == C - 1 else y_steps, 1)
                wait_drained(dve, "TY", j)
                nc.vector.tensor_copy(y_hi[:], turned[:]).then_inc(y_steps, 1)
                dve.wait_ge(y_steps, 2 * (j + 1))
                nc.vector.tensor_tensor(y_lo[:], turned[:], y_hi[:].bitcast(F32), ALU.subtract).then_inc(y_split, 1)

            def gelu_hi(j, i):
                wait_drained(dve, "H1", j, i)
                n = SLICES * j + i
                if n >= 2:
                    wait_hid_used(dve, n - 2)
                nc.vector.tensor_copy(hid_hi[:, i % 2], gelu_raw[:, i % 2]).then_inc(hid_hi_done, 1)

            def finish(j):
                g = j % PAIRS
                dve.wait_ge(mlp_full, j + 1)
                dve.wait_ge(out_base, j + 1)
                xg = x_sb[:, 2 * g:2 * g + 2, :].rearrange("p t n -> p (t n)")
                nc.vector.tensor_tensor(xg, mlp_bank[:], xg, ALU.add).then_inc(mlp_drained, 1)

            dve.wait_ge(consts_in, 48)
            input_norm(0)
            input_norm_apply(0)
            ctx_parts(0)
            weights_lo(0, 1)
            input_parts(0)
            weights_lo(1, 3)
            query_parts(0)
            key_lo(0, 0)
            input_norm(1)
            setup_masks()
            input_norm_apply(1)
            ctx_parts(1)
            input_parts(1)
            weights_lo(3, 5)
            maxima(0, 0)
            maxima(0, 1)
            for j in range(JOBS):
                more, two = j + 1 < JOBS, j + 1 < JOBS and sources(j + 1) == 2
                mlp = j > 0
                normed = j + 2 < PAIRS
                max_rows(j, 0)
                if more:
                    query_parts(j + 1)
                max_rows(j, 1)
                if more:
                    key_lo(j + 1, 0)
                if two:
                    key_lo(j + 1, 1)
                if normed:
                    input_norm(j + 2)
                take_heads(j, 0)
                if normed:
                    input_norm_apply(j + 2)
                take_heads(j, 1)
                normalise_heads(j, 0)
                if mlp:
                    gelu_hi(j - 1, 0)
                normalise_heads(j, 1)
                if mlp:
                    gelu_hi(j - 1, 1)
                out_lo(j)
                if mlp:
                    gelu_hi(j - 1, 2)
                residual(j)
                hidden_moments(j)
                if mlp:
                    gelu_hi(j - 1, 3)
                hidden_norm(j)
                hidden_parts(j)
                if mlp:
                    finish(j - 1)
                if j + 2 < JOBS:
                    ctx_parts(j + 2)
                    input_parts(j + 2)
                if j == 0:
                    weights_lo(5, FIRST_L1)
                if more:
                    maxima(j + 1, 0)
                    maxima(j + 1, 1)
            for i in range(SLICES):
                gelu_hi(JOBS - 1, i)
            finish(JOBS - 1)

        @block.gpsimd
        def _(pool):
            nc.gpsimd.memset(minus_half[:], -0.5).then_inc(consts_set, 1)
            pool.wait_ge(consts_set, 1)
            nc.gpsimd.memset(k_stack[MASK_ROW:MASK_ROW + 2].bitcast(F32), 1.0).then_inc(consts_set, 1)
            pool.wait_ge(consts_set, 2)
            nc.gpsimd.memset(k_stack[MASK_ROW:MASK_ROW + 1, 1].bitcast(F32), 0.0).then_inc(ones_set, 1)
            pool.wait_ge(ones_set, 1)
            nc.gpsimd.memset(q_stack[MASK_ROW:MASK_ROW + 2].bitcast(F32), 1.0).then_inc(ones_set, 1)
            pool.wait_ge(ones_set, 2)
            nc.gpsimd.memset(v_ones[:], 0.0).then_inc(ones_set, 1)
            pool.wait_ge(ones_set, 3)
            nc.gpsimd.memset(v_ones[:, :, :, :, HD:HD + 1], 1.0).then_inc(ones_set, 1)
            pool.wait_ge(ones_set, 4)

            def input_rstd(j):
                pool.wait_ge(x_moments, 6 * (j + 1))
                nc.gpsimd.tensor_tensor(rstd_in[:], spread_in[:], minus_half[:], ALU.pow).then_inc(x_rstd, 1)

            def residual_base(j):
                g = j % PAIRS
                if j > 0:
                    pool.wait_ge(h_normed, 2 * j)
                    pool.wait_ge(out_base, j)
                if layer(j) == 1:
                    pool.wait_ge(mlp_drained, g + 1)
                else:
                    pool.wait_ge(x_in[g], 16)
                for t in range(2):
                    ins = nc.gpsimd.tensor_tensor(h_res[:, t, :], x_sb[:, 2 * g + t, :], bias_rows[:, 2 * layer(j), :], ALU.add)
                    ins.then_inc(res_base if t else pool_half, 1)

            def hidden_rstd(j):
                pool.wait_ge(ln_steps, j + 1)
                nc.gpsimd.tensor_tensor(rstd[:], spread[:], minus_half[:], ALU.pow).then_inc(rstd_done, 1)

            def output_base(j):
                g = j % PAIRS
                wait_drained(pool, "OUT", j)
                if layer(j) == 1:
                    pool.wait_ge(res_base, j + 1)
                for t in range(2):
                    src = h_res[:, t, :] if layer(j) == 0 else x_sb[:, 2 * g + t, :]
                    ins = nc.gpsimd.tensor_tensor(x_sb[:, 2 * g + t, :], src, bias_rows[:, 2 * layer(j) + 1, :], ALU.add)
                    ins.then_inc(out_base if t else pool_half, 1)

            def weights_lo(first, last):
                for n in range(first, last):
                    pool.wait_ge(w_hi_done, n + 1)
                    s = CHUNK_SLOT[n]
                    nc.gpsimd.tensor_tensor(w_lo[:, s].rearrange("p a b -> p (a b)"), w_raw[:, n % W_RING, :],
                                            w_hi[:, s].rearrange("p a b -> p (a b)").bitcast(F32), ALU.subtract).then_inc(w_lo_pool, 1)

            def gelu_lo(j, i):
                pool.wait_ge(hid_hi_done, SLICES * j + i + 1)
                nc.gpsimd.tensor_tensor(hid_lo[:, i % 2], gelu_raw[:, i % 2], hid_hi[:, i % 2].bitcast(F32),
                                        ALU.subtract).then_inc(hid_split, 1)

            input_rstd(0)
            input_rstd(1)
            pool.wait_ge(consts_in, 48)
            for j in range(JOBS):
                mlp = j > 0
                residual_base(j)
                if j + 2 < PAIRS:
                    input_rstd(j + 2)
                if j == 2:
                    weights_lo(FIRST_L1, FIRST_L1_MLP)
                if mlp:
                    gelu_lo(j - 1, 0)
                    gelu_lo(j - 1, 1)
                    gelu_lo(j - 1, 2)
                hidden_rstd(j)
                if mlp:
                    gelu_lo(j - 1, 3)
                output_base(j)
                if j == PAIRS:
                    weights_lo(FIRST_L1_MLP, len(CHUNK_SLOT))
            for i in range(SLICES):
                gelu_lo(JOBS - 1, i)


def kernel(**inputs):
    import numpy as np
    import concourse.bacc as bacc
    from concourse.bass_utils import run_bass_kernel_spmd

    a = {k: np.asarray(v) for k, v in inputs.items()}
    l0 = lambda n: a["L0_xattn_" + n]
    l1 = lambda n: a["L1_xattn_" + n]

    def square(w):
        return w.reshape(C, P, D).transpose(1, 0, 2).reshape(1, P, C * D)

    def wide(w):
        return w.reshape(C, P, SLICES, D).transpose(2, 1, 0, 3).reshape(SLICES, P, C * D)

    def tall(w):
        return w.reshape(SLICES, 2, P, D).transpose(0, 2, 1, 3).reshape(SLICES, P, 2 * D)

    def mlp(up, down):
        return np.stack([wide(up), tall(down)], axis=1).reshape(2 * SLICES, P, 2 * D)

    kv = l1("kv_w").reshape(D, D, 2)
    weights = np.concatenate([square(l0("q_w")), square(l0("k_w")), square(l0("v_w")), square(l0("cproj_w")),
                              mlp(l0("fc_w"), l0("proj_w")),
                              square(l1("q_w")), square(kv[:, :, 0]), square(kv[:, :, 1]), square(l1("out_w")),
                              mlp(l1("mlp_w1"), l1("mlp_w2"))])

    def cols(v):
        return v.reshape(-1, P).T

    kvb = l1("kv_b").reshape(D, 2)
    zero, one = np.zeros(D, np.float32), np.ones(D, np.float32)
    head = (np.arange(P) // HD) % 2
    parity = np.stack([head == 0, head == 1], axis=1).astype(np.float32)
    vectors = np.concatenate(
        [cols(v) for v in (l0("ln1_w"), l0("ln1_b"), l0("q_b"), l0("k_b"), l0("v_b"), l0("ln2_w"), l0("ln2_b"), l0("fc_b"))]
        + [cols(v) for v in (one, zero, l1("q_b"), kvb[:, 0], kvb[:, 1], l1("postnorm_w"), zero, l1("mlp_b1"))]
        + [parity], axis=1)
    arrays = {
        "x": a["x"],
        "ctxT": a["ctx_2048"].reshape(PAIRS, T, C, P).transpose(0, 3, 2, 1),
        "weights": weights,
        "vectors": vectors,
        "rows": np.stack([l0("cproj_b"), l0("proj_b"), l1("out_b"), l1("mlp_b2")]),
        "ident": np.eye(P, dtype=np.float32),
        "mask1": a["mask_BxS2_bf1"].view(np.uint8),
        "mask2": a["mask_BxS2_ik0"],
    }
    arrays = {k: np.ascontiguousarray(v) for k, v in arrays.items()}
    nc = bacc.Bacc("TRN2", target_bir_lowering=False, num_devices=1)
    args = [nc.dram_tensor(k, v.shape, mybir.dt.from_np(v.dtype), kind="ExternalInput").ap() for k, v in arrays.items()]
    args.append(nc.dram_tensor("out", (B, P, D), F32, kind="ExternalOutput").ap())
    xattn_kernel(nc, *args)
    r = run_bass_kernel_spmd(nc, [arrays], core_ids=[0])
    return r.results[0]["out"]
```

```python
from contextlib import ExitStack

import concourse.bass as bass
from concourse import mybir

F32 = mybir.dt.float32
F32R = mybir.dt.float32r
ALU = mybir.AluOpType
ACT = mybir.ActivationFunctionType
AX = mybir.AxisListType

P = 128
B = 8
D = 256
C = D // P
H = 16
HD = D // H
PAIRS = B // 2
T = 2 * P
JOBS = 2 * PAIRS
SLICES = 4
QUADS = H // 4
MASK_ROW, MAX_ROW = 96, 97
BIG = float(2.0 ** 100)
EPS = (1e-5, 1e-6)
SCALE = (0.25, 1.0 / 16.0)

RING = 6
W_RING = 6
PT_RING = 4
LAG = 3

WQ, WK, WV, WO = range(4)
W_FC, W_PROJ = 8, 12
CHUNK_SLOT = [0, 1, 2, 3, 8, 12, 9, 13, 10, 14, 11, 15, 4, 5, 6, 7, 8, 9, 10, 11, 12, 13, 14, 15]
FIRST_L1, FIRST_L1_MLP, LAST_PROJ = 12, 16, 22

V_INW, V_INB, V_QB, V_KB, V_VB, V_NW, V_NB, V_FCB = 0, 2, 4, 6, 8, 10, 12, 14
V_LAYER = 22
V_PARITY = 2 * V_LAYER
V_COLS = V_PARITY + 2


def layer(j):
    return j // PAIRS


def sources(j):
    return 1 + layer(j)


def k_bursts_before(j):
    return sum(sources(i) for i in range(j))


def latents_before(j):
    return sum(layer(i) for i in range(j))


def ctx_slot(j):
    return 1 + j % 2


def score_bursts(j, b, half=None):
    n = QUADS * sources(j)
    names = [("S", j, b, i) for i in range(n)]
    return names if half is None else names[half * n // 2:(half + 1) * n // 2]


def max_turn(j):
    return 2 * sources(j)


def burst_order():
    order = [("TI", 0), ("Q", 0), ("K", 0, 0), ("V", 0, 0), ("TI", 1)]
    for j in range(JOBS):
        more, two = j + 1 < JOBS, j + 1 < JOBS and sources(j + 1) == 2
        shifted = [[("ST", j, b, i) for i in range(QUADS * sources(j))] for b in range(2)]
        half = max_turn(j)
        early = not more
        order += score_bursts(j, 0)
        order += [("Q", j + 1)] if more else []
        order += [("H1", j - 1, 0)] if early else []
        order += [("TM", j, 0)]
        order += score_bursts(j, 1, 0)
        order += [("K", j + 1, 0)] if more else []
        order += [("H1", j - 1, 1)] if early else []
        order += score_bursts(j, 1, 1)
        order += [("K", j + 1, 1)] if two else []
        order += shifted[0][:half] + [("TM", j, 1)] + shifted[0][half:] + shifted[1]
        order += [("TO", j, 0)]
        order += [("H1", j - 1, 0)] if j > 0 and not early else []
        order += [("TO", j, 1)]
        order += [("H1", j - 1, 1)] if j > 0 and not early else []
        order += [("V", j + 1, 0)] if two else []
        order += [("TOT", j)]
        order += [("H1", j - 1, 2)] if j > 0 else []
        order += [("OUT", j)]
        order += [("H1", j - 1, 3)] if j > 0 else []
        order += [("TI", j + 2)] if j + 2 < JOBS else []
        order += [("V", j + 1, sources(j + 1) - 1)] if more else []
        order += [("TY", j)]
    order += [("H1", JOBS - 1, i) for i in range(SLICES)]
    return order


def xattn_kernel(nc, x, ctxT, weights, vectors, rows, ident, mask1, mask2, out):
    number = {name: n for n, name in enumerate(burst_order())}
    exp_number = {}
    for j in range(JOBS):
        for b in range(2):
            for i in range(QUADS * sources(j)):
                exp_number[j, b, i] = len(exp_number)

    with ExitStack() as ctx:
        def sb(name, shape, dt=F32):
            return ctx.enter_context(nc.sbuf_tensor(name, shape, dt))

        def sem(name):
            return ctx.enter_context(nc.semaphore(name))

        x_sb = sb("x_sb", [P, B, D])
        ctx_raw = sb("ctx_raw", [P, C, T])
        ctx_hi = sb("ctx_hi", [P, C, T], F32R)
        ctx_lo = sb("ctx_lo", [P, C, T], F32R)
        spread_in = sb("spread_in", [P, 2])
        x_norm = sb("x_norm", [P, 2, D])
        turned = sb("turned", [P, C, T])
        in_hi = sb("in_hi", [P, C, T], F32R)
        in_lo = sb("in_lo", [P, C, T], F32R)
        q_raw = sb("q_raw", [P, C, T])
        q_hi = sb("q_hi", [P, 2, C, T], F32R)
        q_lo = sb("q_lo", [P, 2, C, T], F32R)
        k_hi = sb("k_hi", [P, 2, C, T], F32R)
        k_lo = sb("k_lo", [P, 2, C, T], F32R)
        q_stack = sb("q_stack", [P, 4, 2, C, T], F32R)
        k_stack = sb("k_stack", [P, 3, 4, C, T], F32R)
        v_ones = sb("v_ones", [P, 2, 2, H, 32])
        probs = sb("probs", [P, PT_RING, 4 * P])
        neg_max = sb("neg_max", [P, 2, H])
        neg_maxT = sb("neg_maxT", [H, 2, P], F32R)
        o_raw = sb("o_raw", [P, 2, QUADS * P])
        o_recip = sb("o_recip", [P, 2, H])
        normed = sb("normed", [P, 2, D])
        oT_hi = sb("oT_hi", [P, C, T], F32R)
        oT_lo = sb("oT_lo", [P, C, T], F32R)
        h_res = sb("h_res", [P, 2, D])
        y_hi = sb("y_hi", [P, C, T], F32R)
        y_lo = sb("y_lo", [P, C, T], F32R)
        gelu_raw = sb("gelu_raw", [P, 2, 2, T])
        hid_hi = sb("hid_hi", [P, 2, 2, T], F32R)
        hid_lo = sb("hid_lo", [P, 2, 2, T], F32R)
        w_raw = sb("w_raw", [P, W_RING, 2 * D])
        w_hi = sb("w_hi", [P, 16, 2, D], F32R)
        w_lo = sb("w_lo", [P, 16, 2, D], F32R)
        vec = sb("vec", [P, V_COLS])
        bias_rows = sb("bias_rows", [P, 4, D])
        ident_sb = sb("ident_sb", [P, P])
        stats_in = sb("stats_in", [P, 2, 6])
        moments_in = sb("moments_in", [P, 2, 2])
        rstd_in = sb("rstd_in", [P, 2])
        stats = sb("stats", [P, 2, 6])
        moments = sb("moments", [P, 2, 2])
        spread = sb("spread", [P, 2])
        rstd = sb("rstd", [P, 2])
        table_tmp = sb("table_tmp", [P, 2])
        minus_half = sb("minus_half", [P, 2])
        mask1_all = gelu_raw[:, 0].rearrange("p f n -> p (f n)")[:, 0:B * P // 4].bitcast(mybir.dt.uint8)
        mask1_sb = sb("mask1_sb", [B, P], mybir.dt.uint8)
        mask2_sb = gelu_raw[0:B, 1, 0, 0:P].bitcast(mybir.dt.int32)
        mask_any = sb("mask_any", [B, 1])
        mask_tmp = gelu_raw[0:B, 1, 0, P:2 * P]
        mask_bias = sb("mask_bias", [B, 2, P], F32R)
        scale0 = sb("scale0", [P, B])

        banks = [ctx.enter_context(nc.psum_tensor(f"bank{i}", [P, 512], F32)) for i in range(RING)]
        o_bank = ctx.enter_context(nc.psum_tensor("o_bank", [P, 512], F32))
        mlp_bank = ctx.enter_context(nc.psum_tensor("mlp_bank", [P, 512], F32))

        bank_full = [sem(f"bank_full{i}") for i in range(RING)]
        bank_drained = [sem(f"bank_drained{i}") for i in range(RING)]
        o_full, o_drained = sem("o_full"), sem("o_drained")
        mlp_full, mlp_drained = sem("mlp_full"), sem("mlp_drained")
        x_in = [sem(f"x_in{g}") for g in range(PAIRS)]
        ctx_in, consts_in, biases_in, masks_in = sem("ctx_in"), sem("consts_in"), sem("biases_in"), sem("masks_in")
        w_in = [sem(f"w_in{i}") for i in range(W_RING)]
        w_hi_done, w_lo_dve, w_lo_pool = sem("w_hi_done"), sem("w_lo_dve"), sem("w_lo_pool")
        v_set = sem("v_set")
        consts_set, ones_set, masks_set = sem("consts_set"), sem("ones_set"), sem("masks_set")
        ctx_hi_done, ctx_split = sem("ctx_hi_done"), sem("ctx_split")
        x_moments, x_rstd, x_normed = sem("x_moments"), sem("x_rstd"), sem("x_normed")
        in_steps, in_hi_done, in_split = sem("in_steps"), sem("in_hi_done"), sem("in_split")
        q_raw_done, q_split = sem("q_raw_done"), sem("q_split")
        k_hi_done, k_lo_half = sem("k_hi_done"), sem("k_lo_half")
        q_stacked, ctx_stacked, latents_stacked = sem("q_stacked"), sem("ctx_stacked"), sem("latents_stacked")
        max_stacked = [sem(f"max_stacked{b}") for b in range(2)]
        q_stacked_pool, latents_stacked_pool = sem("q_stacked_pool"), sem("latents_stacked_pool")
        probs_used = sem("probs_used")
        recip_done = sem("recip_done")
        table_step = sem("table_step")
        q_copied, k_copied = sem("q_copied"), sem("k_copied")
        oT_hi_done, oT_lo_half = sem("oT_hi_done"), sem("oT_lo_half")
        res_base, out_base = sem("res_base"), sem("out_base")
        ln_steps, rstd_done, h_normed = sem("ln_steps"), sem("rstd_done"), sem("h_normed")
        y_steps, y_hi_done, y_split = sem("y_steps"), sem("y_hi_done"), sem("y_split")
        gelu_done, hid_hi_done, hid_split, hid_used = sem("gelu_done"), sem("hid_hi_done"), sem("hid_split"), sem("hid_used")
        stored = sem("stored")
        pool_half = sem("pool_half")
        dve_step = sem("dve_step")

        def wait_full(eng, *name):
            n = number[name]
            eng.wait_ge(bank_full[n % RING], n // RING + 1)
            return banks[n % RING]

        def wait_drained(eng, *name):
            n = number[name]
            eng.wait_ge(bank_drained[n % RING], n // RING + 1)

        def drained(*name):
            return bank_drained[number[name] % RING]

        def wait_probs_used(eng, m):
            for (j, b, i), k in exp_number.items():
                if k == m:
                    if i == QUADS * sources(j) - 1:
                        eng.wait_ge(o_full, 2 * j + b + 1)
                    else:
                        eng.wait_ge(probs_used, m + 1 - (2 * j + b))

        def wait_hid_used(eng, n):
            j, i = n // SLICES, n % SLICES
            if i == SLICES - 1:
                eng.wait_ge(mlp_full, j + 1)
            else:
                eng.wait_ge(hid_used, (SLICES - 1) * j + i + 1)

        def col(ell, first, c):
            k = ell * V_LAYER + first + c
            return vec[:, k:k + 1]

        block = ctx.enter_context(nc.Block())

        @block.sync
        def _(sp):
            def load_weights(first, last):
                for n in range(first, last):
                    if n >= W_RING:
                        m = n - W_RING
                        if m < FIRST_L1:
                            sp.wait_ge(w_lo_dve, m + 1)
                        else:
                            sp.wait_ge(w_lo_pool, m + 1 - FIRST_L1)
                    sp.dma_start(w_raw[:, n % W_RING, :], weights[n]).then_inc(w_in[n % W_RING], 16)

            def load_ctx(j):
                if j > 0:
                    sp.wait_ge(ctx_split, j)
                sp.dma_start(ctx_raw[:], ctxT[j % PAIRS]).then_inc(ctx_in, 16)

            def load_x(g):
                sp.dma_start(x_sb[:, 2 * g:2 * g + 2, :], x[2 * g:2 * g + 2].rearrange("b p n -> p b n")).then_inc(x_in[g], 16)

            def stack_rows(stack, parts, done):
                for r, part in enumerate(parts):
                    for p in range(4):
                        sp.dma_start(stack[32 * r:32 * r + 32, p].bitcast(F32), part[32 * p:32 * p + 32].bitcast(F32)).then_inc(done, 16)

            def stack_context(j):
                slot = ctx_slot(j)
                if j > 1:
                    sp.wait_ge(o_full, 2 * (j - 1))
                wait_drained(sp, "K", j, 0)
                if j > 0:
                    stack_rows(k_stack[:, slot], (k_hi[:, 0], k_hi[:, 0], k_lo[:, 0]), ctx_stacked)
                else:
                    for p in range(4):
                        sp.dma_start(k_stack[64:96, slot, p].bitcast(F32), k_lo[32 * p:32 * p + 32, 0].bitcast(F32)).then_inc(ctx_stacked, 16)
                    sp.wait_ge(masks_set, 4)
                    sp.wait_ge(ones_set, 3)
                for b in range(2):
                    dst = k_stack[MASK_ROW:MASK_ROW + 1, slot, :, :, b * P:b * P + P].rearrange("o p c n -> o (p c) n")
                    batch = 2 * (j % PAIRS) + b
                    src = mask_bias[batch:batch + 1, layer(j):layer(j) + 1, :].bitcast(F32)
                    sp.dma_start(dst.bitcast(F32), src.to_broadcast([1, 4 * C, P])).then_inc(ctx_stacked, 16)

            def stack_queries(j):
                sp.wait_ge(o_full, 2 * j)
                sp.wait_ge(q_split, 4 * (j + 1))
                stack_rows(q_stack, (q_hi, q_lo, q_hi), q_stacked)

            def stack_latents(j):
                wait_drained(sp, "K", j, 1)
                stack_rows(k_stack[:, 0], (k_hi[:, 1],), latents_stacked)

            def store(g):
                sp.wait_ge(mlp_drained, PAIRS + g + 1)
                sp.dma_start(out[2 * g:2 * g + 2].rearrange("b p n -> p b n"), x_sb[:, 2 * g:2 * g + 2, :]).then_inc(stored, 16)

            load_x(0)
            sp.dma_start(vec[:], vectors).then_inc(consts_in, 16)
            sp.dma_start(ident_sb[:], ident).then_inc(consts_in, 16)
            load_ctx(0)
            load_weights(0, 3)
            sp.dma_start(mask1_sb[:], mask1).then_inc(masks_in, 16)
            sp.dma_start(mask2_sb, mask2).then_inc(masks_in, 16)
            sp.dma_start(mask1_all, mask1.rearrange("b n -> (b n)").partition_broadcast(P)).then_inc(masks_in, 16)
            sp.dma_start(bias_rows[:], rows.rearrange("r n -> (r n)").partition_broadcast(P)).then_inc(biases_in, 16)
            load_x(1)
            load_ctx(1)
            load_weights(3, 3 + W_RING)
            stack_context(0)
            load_x(2)
            load_x(3)
            for j in range(JOBS):
                if j + 2 < JOBS:
                    load_ctx(j + 2)
                if j + 1 < JOBS:
                    stack_context(j + 1)
                if j == 0:
                    load_weights(3 + W_RING, FIRST_L1)
                if j == PAIRS + 1:
                    load_weights(FIRST_L1_MLP + W_RING, len(CHUNK_SLOT))
                if j + 1 < JOBS:
                    stack_queries(j + 1)
                    if layer(j + 1) == 1:
                        stack_latents(j + 1)
                if j == 1:
                    load_weights(FIRST_L1, FIRST_L1_MLP)
                if j == 2:
                    load_weights(FIRST_L1_MLP, FIRST_L1_MLP + W_RING)
                if j > PAIRS + 1:
                    store(j - PAIRS - 2)
            store(PAIRS - 2)
            store(PAIRS - 1)
            sp.wait_ge(stored, 16 * PAIRS)

        @block.tensor
        def _(pe):
            opened = [0]

            def take_bank(*name):
                n = number[name]
                assert n == opened[0], (name, n, opened[0])
                opened[0] += 1
                if n >= RING:
                    pe.wait_ge(bank_drained[n % RING], n // RING)
                return banks[n % RING], bank_full[n % RING]

            def product(dst, a_hi, a_lo, b_hi, b_lo, first, last, shared=False):
                parts = [(a_hi, b_hi), (a_hi, b_lo), (a_lo, b_hi)]
                for k, (a, m) in enumerate(parts):
                    mm = pe.matmul(dst, a, m, start=first and k == 0, stop=last and k == 2, skip_group_check=shared)
                return mm

            def weight(slot, k, cols):
                return w_hi[:, slot, k, cols], w_lo[:, slot, k, cols]

            def wait_weights(upto):
                if upto <= FIRST_L1:
                    pe.wait_ge(w_lo_dve, upto)
                else:
                    pe.wait_ge(w_lo_pool, upto - FIRST_L1)

            def features(name, slot, hi, lo):
                bank, full = take_bank(*name)
                for m in range(C):
                    for k in range(C):
                        a = weight(slot, k, slice(m * P, m * P + P))
                        mm = product(bank[:, m * T:m * T + T], *a, hi[:, k, :], lo[:, k, :], k == 0, k == C - 1)
                mm.then_inc(full, 1)

            def tokens(name, slot, hi, lo):
                bank, full = take_bank(*name)
                for t in range(2):
                    for k in range(C):
                        cols = slice(t * P, t * P + P)
                        mm = product(bank[:, t * D:t * D + D], hi[:, k, cols], lo[:, k, cols],
                                     *weight(slot, k, slice(0, D)), k == 0, k == C - 1)
                mm.then_inc(full, 1)

            def turn_tokens(name, src):
                bank, full = take_bank(*name)
                for c in range(C):
                    for t in range(2):
                        mm = pe.transpose(bank[:, c * T + t * P:c * T + t * P + P], src[:, t, c * P:c * P + P], ident_sb[:])
                mm.then_inc(full, 1)

            def turn_inputs(j):
                if layer(j) == 0:
                    pe.wait_ge(x_normed, 2 * (j + 1))
                    turn_tokens(("TI", j), x_norm)
                else:
                    g = j % PAIRS
                    pe.wait_ge(mlp_drained, g + 1)
                    turn_tokens(("TI", j), x_sb[:, 2 * g:2 * g + 2, :])

            def queries(j):
                pe.wait_ge(in_split, j + 1)
                wait_weights((0 if layer(j) == 0 else FIRST_L1) + WQ + 1)
                features(("Q", j), 4 * layer(j) + WQ, in_hi, in_lo)

            def keys(j, s):
                if s == 0:
                    pe.wait_ge(ctx_split, j + 1)
                wait_weights((0 if layer(j) == 0 else FIRST_L1) + WK + 1)
                features(("K", j, s), 4 * layer(j) + WK, *((in_hi, in_lo) if s else (ctx_hi, ctx_lo)))

            def values(j, s):
                wait_weights((0 if layer(j) == 0 else FIRST_L1) + WV + 1)
                tokens(("V", j, s), 4 * layer(j) + WV, *((in_hi, in_lo) if s else (ctx_hi, ctx_lo)))

            def scores(j, b, half):
                n = sources(j)
                if b == 0 and half == 0:
                    if j == 0:
                        pe.wait_ge(q_copied, 8)
                        pe.wait_ge(q_stacked_pool, 16 * 4)
                        pe.wait_ge(k_copied, 8)
                    else:
                        pe.wait_ge(q_stacked, 16 * 12 * j)
                    pe.wait_ge(ctx_stacked, 16 * (14 * j + 6))
                    if n == 2:
                        pe.wait_ge(latents_stacked, 16 * 4 * latents_before(j + 1))
                        pe.wait_ge(latents_stacked_pool, 16 * 8 * latents_before(j + 1))
                cols = slice(b * P, b * P + P)
                rows_ = slice(0, MASK_ROW + 1)
                slot = ctx_slot(j)
                slots = slice(slot, slot + 1) if n == 1 else slice(0, slot + 1, slot)
                for name in score_bursts(j, b, half):
                    bank, full = take_bank(*name)
                    i = name[3]
                    pairs = (2 * (i % 2), 2 * (i % 2) + 1) if n == 1 else (i % 4,)
                    c = i // 2 if n == 1 else i // 4
                    for k, p in enumerate(pairs):
                        for e in range(2):
                            at = (2 * k + e) * n * P
                            mm = pe.matmul(bank[:, at:at + n * P], q_stack[rows_, p, e, c, cols],
                                           k_stack[rows_, slots, p, c, cols], start=True, stop=True)
                    mm.then_inc(full, 1)

            def turn_max(j, b):
                wait_drained(pe, *score_bursts(j, b)[-1])
                bank, full = take_bank("TM", j, b)
                pe.transpose(bank[0:H, 0:P], neg_max[:, b, :], ident_sb[:]).then_inc(full, 1)

            def attend(j, b):
                n = sources(j)
                cols = slice(b * P, b * P + P)
                pe.wait_ge(max_stacked[b], 16 * (j + 1))

                def shifted(i):
                    quad, s = i // n, i % n
                    bank, full = take_bank("ST", j, b, i)
                    for k in range(2):
                        p = 2 * (quad % 2) + k
                        mm = pe.matmul(bank[:, k * T:k * T + T], k_stack[0:MAX_ROW + 1, 0 if s else ctx_slot(j), p, quad // 2, cols],
                                       q_stack[0:MAX_ROW + 1, p, :, quad // 2, cols], start=True, stop=True)
                    mm.then_inc(full, 1)

                def weigh(i):
                    quad, s = i // n, i % n
                    wait_drained(pe, "ST", j, b, i)
                    if i == 0:
                        if b == 0:
                            wait_drained(pe, "V", j, n - 1)
                        if 2 * j + b > 0:
                            pe.wait_ge(o_drained, 2 * j + b)
                    slot = exp_number[j, b, i] % PT_RING
                    for h in range(4):
                        mm = pe.matmul(o_bank[32 * h:32 * h + 32, quad * P:quad * P + P],
                                       v_ones[:, b, s, 4 * quad + h, :], probs[:, slot, h * P:h * P + P],
                                       start=s == 0, stop=s == n - 1)
                    if i == QUADS * n - 1:
                        mm.then_inc(o_full, 1)
                    else:
                        mm.then_inc(probs_used, 1)

                last = QUADS * n
                for i in range(last + LAG):
                    if b == 0 and i == max_turn(j):
                        turn_max(j, 1)
                        if j > 1 and (n == 1 or j + 1 < JOBS):
                            mlp_down(j - 2, 2 if n == 1 else 3)
                    if i < last:
                        shifted(i)
                    if b == 1 and i == LAG - 1 and j > 1 and n == 1:
                        mlp_down(j - 2, 3)
                    if i >= LAG:
                        weigh(i - LAG)

            def turn_out(j, b):
                pe.wait_ge(o_drained, 2 * j + b + 1)
                bank, full = take_bank("TO", j, b)
                for i in range(QUADS):
                    mm = pe.transpose(bank[:, i * P:i * P + P], o_raw[:, b, i * P:i * P + P], ident_sb[:])
                mm.then_inc(full, 1)

            def turn_back(j):
                wait_drained(pe, "TO", j, 0)
                wait_drained(pe, "TO", j, 1)
                turn_tokens(("TOT", j), normed)

            def attention_out(j):
                wait_drained(pe, "TOT", j)
                if j == 0:
                    wait_weights(WO + 1)
                tokens(("OUT", j), 4 * layer(j) + WO, oT_hi, oT_lo)

            def turn_hidden(j):
                pe.wait_ge(h_normed, 2 * (j + 1))
                turn_tokens(("TY", j), normed)

            def mlp_up(j, i):
                if i == 0:
                    pe.wait_ge(y_split, j + 1)
                if j in (0, PAIRS):
                    wait_weights(4 + 2 * i + 1 if j == 0 else FIRST_L1_MLP + i + 1)
                features(("H1", j, i), W_FC + i, y_hi, y_lo)

            def mlp_down(j, i):
                pe.wait_ge(hid_split, SLICES * j + i + 1)
                if i == 0 and j > 0:
                    pe.wait_ge(mlp_drained, j)
                if j in (0, PAIRS):
                    wait_weights(4 + 2 * i + 2 if j == 0 else FIRST_L1_MLP + SLICES + i + 1)
                for k in range(2):
                    for t in range(2):
                        a = (hid_hi[:, i % 2, k, t * P:t * P + P], hid_lo[:, i % 2, k, t * P:t * P + P])
                        mm = product(mlp_bank[:, t * D:t * D + D], *a, *weight(W_PROJ + i, k, slice(0, D)),
                                     i == 0 and k == 0 and t == 0, i == SLICES - 1 and k == 1, shared=True)
                mm.then_inc(mlp_full if i == SLICES - 1 else hid_used, 1)

            pe.wait_ge(consts_in, 32)
            turn_inputs(0)
            queries(0)
            keys(0, 0)
            values(0, 0)
            turn_inputs(1)
            for j in range(JOBS):
                more, two = j + 1 < JOBS, j + 1 < JOBS and sources(j + 1) == 2
                mlp = j > 0
                early = not more
                scores(j, 0, 0)
                if j > 1 and layer(j) == 1:
                    mlp_down(j - 2, 2)
                scores(j, 0, 1)
                if j + 1 == JOBS:
                    mlp_down(j - 2, 3)
                if more:
                    queries(j + 1)
                if early:
                    mlp_up(j - 1, 0)
                turn_max(j, 0)
                scores(j, 1, 0)
                if more:
                    keys(j + 1, 0)
                if early:
                    mlp_up(j - 1, 1)
                scores(j, 1, 1)
                if two:
                    keys(j + 1, 1)
                attend(j, 0)
                attend(j, 1)
                turn_out(j, 0)
                if mlp and not early:
                    mlp_up(j - 1, 0)
                turn_out(j, 1)
                if mlp and not early:
                    mlp_up(j - 1, 1)
                if two:
                    values(j + 1, 0)
                if early:
                    mlp_down(j - 1, 0)
                turn_back(j)
                if mlp:
                    if not early:
                        mlp_down(j - 1, 0)
                    mlp_up(j - 1, 2)
                attention_out(j)
                if mlp:
                    mlp_down(j - 1, 1)
                    mlp_up(j - 1, 3)
                if j + 2 < JOBS:
                    turn_inputs(j + 2)
                if more:
                    values(j + 1, sources(j + 1) - 1)
                if early:
                    mlp_down(j - 1, 2)
                turn_hidden(j)
                if early:
                    mlp_down(j - 1, 3)
            last = JOBS - 1
            mlp_up(last, 0)
            mlp_up(last, 1)
            mlp_down(last, 0)
            mlp_up(last, 2)
            mlp_down(last, 1)
            mlp_up(last, 3)
            mlp_down(last, 2)
            mlp_down(last, 3)

        @block.scalar
        def _(act):
            def weights_hi(first, last):
                for n in range(first, last):
                    act.wait_ge(w_in[n % W_RING], 16 * (n // W_RING + 1))
                    if n == FIRST_L1_MLP:
                        wait_full(act, "H1", PAIRS - 1, SLICES - 1)
                    if n == LAST_PROJ:
                        act.wait_ge(mlp_full, PAIRS)
                    nc.scalar.activation(w_hi[:, CHUNK_SLOT[n]].rearrange("p a b -> p (a b)"), w_raw[:, n % W_RING, :],
                                         ACT.Copy).then_inc(w_hi_done, 1)

            def ctx_parts(j):
                act.wait_ge(ctx_in, 16 * (j + 1))
                if j > 0:
                    wait_full(act, "V", j - 1, 0)
                nc.scalar.activation(ctx_hi[:], ctx_raw[:], ACT.Copy).then_inc(ctx_hi_done, 1)

            def input_hi(j):
                bank = wait_full(act, "TI", j)
                if j > 0:
                    act.wait_ge(in_split, j)
                if j > 2:
                    act.wait_ge(y_split, j - 2)
                for c in range(C):
                    src = bank[:, c * T:c * T + T]
                    ins = nc.scalar.activation(turned[:, c, :], src, ACT.Identity, bias=col(layer(j), V_INB, c), scale=col(layer(j), V_INW, c))
                    ins.then_inc(drained("TI", j) if c == C - 1 else in_steps, 1)
                wait_drained(act, "TI", j)
                act.wait_ge(in_steps, j + 1)
                if j > 0:
                    wait_full(act, "V", j - 1, sources(j - 1) - 1)
                nc.scalar.activation(in_hi[:], turned[:], ACT.Copy).then_inc(in_hi_done, 1)

            def hidden_hi(j):
                bank = wait_full(act, "TY", j)
                act.wait_ge(in_split, min(j + 3, JOBS))
                if j > 0:
                    act.wait_ge(y_split, j)
                for c in range(C):
                    nc.scalar.activation(turned[:, c, :], bank[:, c * T:c * T + T], ACT.Identity, bias=col(layer(j), V_NB, c),
                                         scale=col(layer(j), V_NW, c)).then_inc(drained("TY", j) if c == C - 1 else y_steps, 1)
                wait_drained(act, "TY", j)
                act.wait_ge(y_steps, j + 1)
                nc.scalar.activation(y_hi[:], turned[:], ACT.Copy).then_inc(y_hi_done, 1)

            def query_bias(j):
                bank = wait_full(act, "Q", j)
                if j > 0:
                    act.wait_ge(q_split, 4 * j)
                for c in range(C):
                    nc.scalar.activation(q_raw[:, c, :], bank[:, c * T:c * T + T], ACT.Identity,
                                         bias=col(layer(j), V_QB, c)).then_inc(drained("Q", j) if c == C - 1 else q_raw_done, 1)

            def key_hi(j, s):
                bank = wait_full(act, "K", j, s)
                if j > 0:
                    if s == 0:
                        act.wait_ge(ctx_stacked, 16 * (14 * j - 8))
                        if j == 1:
                            act.wait_ge(k_copied, 8)
                    elif latents_before(j) > 0:
                        act.wait_ge(latents_stacked, 16 * 4 * latents_before(j))
                        act.wait_ge(latents_stacked_pool, 16 * 8 * latents_before(j))
                for c in range(C):
                    nc.scalar.activation(k_hi[:, s, c, :], bank[:, c * T:c * T + T], ACT.Identity,
                                         bias=col(layer(j), V_KB, c)).then_inc(k_hi_done, 1)

            def value_copy(j, s):
                bank = wait_full(act, "V", j, s)
                if j == 0:
                    act.wait_ge(v_set, 2)
                else:
                    act.wait_ge(o_full, 2 * j)
                nc.scalar.activation(v_ones[:, :, s, :, 0:HD], bank[:].rearrange("p (t h d) -> p t h d", t=2, h=H),
                                     ACT.Copy).then_inc(drained("V", j, s), 1)

            def exponentials(j, b):
                n = sources(j)
                for i in range(QUADS * n):
                    bank = wait_full(act, "ST", j, b, i)
                    m = exp_number[j, b, i]
                    if m >= PT_RING:
                        wait_probs_used(act, m - PT_RING)
                    if layer(j) == 0:
                        batch = 2 * (j % PAIRS) + b
                        scale = scale0[:, batch:batch + 1]
                    else:
                        scale = SCALE[1]
                    nc.scalar.activation(probs[:, m % PT_RING, :], bank[:], ACT.Exp, scale=scale).then_inc(drained("ST", j, b, i), 1)

            def out_hi(j):
                bank = wait_full(act, "TOT", j)
                for c in range(C):
                    nc.scalar.activation(oT_hi[:, c, :], bank[:, c * T:c * T + T], ACT.Identity,
                                         bias=col(layer(j), V_VB, c)).then_inc(oT_hi_done, 1)

            def gelu(j, i):
                bank = wait_full(act, "H1", j, i)
                n = SLICES * j + i
                if n >= 2:
                    act.wait_ge(hid_split, n - 1)
                for f in range(2):
                    nc.scalar.activation(gelu_raw[:, i % 2, f, :], bank[:, f * T:f * T + T], ACT.Gelu_apprx_tanh,
                                         bias=col(layer(j), V_FCB, 2 * i + f)).then_inc(drained("H1", j, i) if f else gelu_done, 1)

            act.wait_ge(consts_set, 1)
            nc.scalar.activation(table_tmp[:], minus_half[:], ACT.Exp).then_inc(table_step, 1)
            act.wait_ge(consts_in, 32)
            weights_hi(0, 1)
            ctx_parts(0)
            weights_hi(1, 2)
            input_hi(0)
            weights_hi(2, 3)
            query_bias(0)
            key_hi(0, 0)
            act.wait_ge(k_hi_done, C)
            for r in range(2):
                for p in range(4):
                    nc.scalar.activation(k_stack[32 * r:32 * r + 32, ctx_slot(0), p], k_hi[32 * p:32 * p + 32, 0], ACT.Copy).then_inc(k_copied, 1)
            value_copy(0, 0)
            ctx_parts(1)
            input_hi(1)
            weights_hi(3, 3 + W_RING)
            act.wait_ge(masks_set, 5)
            for j in range(JOBS):
                more, two = j + 1 < JOBS, j + 1 < JOBS and sources(j + 1) == 2
                mlp, early = j > 0, not more
                if early:
                    gelu(j - 1, 0)
                    gelu(j - 1, 1)
                act.wait_ge(table_step, j + 1)
                nc.scalar.activation(table_tmp[:], minus_half[:], ACT.Exp).then_inc(table_step, 1)
                if j == PAIRS + 1:
                    weights_hi(FIRST_L1_MLP, FIRST_L1_MLP + 2)
                if more:
                    query_bias(j + 1)
                if j == PAIRS + 1:
                    weights_hi(FIRST_L1_MLP + 2, FIRST_L1_MLP + 4)
                if more:
                    key_hi(j + 1, 0)
                if j == PAIRS + 1:
                    weights_hi(FIRST_L1_MLP + 4, LAST_PROJ)
                if two:
                    key_hi(j + 1, 1)
                exponentials(j, 0)
                if j == 2:
                    weights_hi(FIRST_L1, FIRST_L1 + 2)
                exponentials(j, 1)
                if j == 2:
                    weights_hi(FIRST_L1 + 2, FIRST_L1_MLP)
                if mlp and not early:
                    gelu(j - 1, 0)
                    gelu(j - 1, 1)
                if two:
                    value_copy(j + 1, 0)
                out_hi(j)
                if j == 0:
                    weights_hi(3 + W_RING, FIRST_L1)
                if j == PAIRS + 1:
                    weights_hi(LAST_PROJ, len(CHUNK_SLOT))
                if mlp:
                    gelu(j - 1, 2)
                    gelu(j - 1, 3)
                if j + 2 < JOBS:
                    input_hi(j + 2)
                if more:
                    value_copy(j + 1, sources(j + 1) - 1)
                if j + 2 < JOBS:
                    ctx_parts(j + 2)
                hidden_hi(j)
            for i in range(SLICES):
                gelu(JOBS - 1, i)

        @block.vector
        def _(dve):
            steps = [0]

            def link(ins):
                steps[0] += 1
                ins.then_inc(dve_step, 1)
                dve.wait_ge(dve_step, steps[0])

            def setup_masks():
                dve.wait_ge(masks_in, 48)
                nc.vector.tensor_reduce(mask_any[:], mask1_sb[:], AX.X, ALU.max).then_inc(masks_set, 1)
                nc.vector.tensor_scalar(mask_tmp, mask1_sb[:], -1.0, BIG, ALU.add, ALU.mult).then_inc(masks_set, 1)
                dve.wait_ge(masks_set, 2)
                nc.vector.tensor_scalar(mask_bias[:, 0, :], mask_tmp, mask_any[:], None, ALU.mult).then_inc(masks_set, 1)
                nc.vector.tensor_scalar(mask_bias[:, 1, :], mask2_sb, 0.0, -BIG, ALU.is_equal, ALU.mult).then_inc(masks_set, 1)
                link(nc.vector.tensor_reduce(scale0[:], mask1_all.rearrange("p (b n) -> p b n", b=B), AX.X, ALU.max))
                nc.vector.tensor_scalar(scale0[:], scale0[:], SCALE[0], None, ALU.mult).then_inc(masks_set, 1)

            def weights_lo(first, last):
                for n in range(first, last):
                    dve.wait_ge(w_hi_done, n + 1)
                    s = CHUNK_SLOT[n]
                    nc.vector.tensor_tensor(w_lo[:, s].rearrange("p a b -> p (a b)"), w_raw[:, n % W_RING, :],
                                            w_hi[:, s].rearrange("p a b -> p (a b)").bitcast(F32), ALU.subtract).then_inc(w_lo_dve, 1)

            def input_norm(j):
                g = j % PAIRS
                dve.wait_ge(x_in[g], 16)
                for t in range(2):
                    nc.vector.bn_stats(stats_in[:, t, :], x_sb[:, 2 * g + t, :]).then_inc(x_moments, 1)
                dve.wait_ge(x_moments, 6 * j + 2)
                if j > 0:
                    dve.wait_ge(x_normed, 2 * j)
                for t in range(2):
                    nc.vector.bn_aggr(moments_in[:, t, :], stats_in[:, t, :]).then_inc(x_moments, 1)
                dve.wait_ge(x_moments, 6 * j + 4)
                if j > 0:
                    dve.wait_ge(x_rstd, j)
                for t in range(2):
                    nc.vector.tensor_scalar(spread_in[:, t:t + 1], moments_in[:, t, 1:2], EPS[0], None, ALU.add).then_inc(x_moments, 1)

            def input_norm_apply(j):
                g = j % PAIRS
                dve.wait_ge(x_rstd, j + 1)
                if j > 0:
                    wait_full(dve, "TI", j - 1)
                for t in range(2):
                    nc.vector.tensor_scalar(x_norm[:, t, :], x_sb[:, 2 * g + t, :], moments_in[:, t, 0:1], rstd_in[:, t:t + 1],
                                            ALU.subtract, ALU.mult).then_inc(x_normed, 1)

            def context_lo(j):
                dve.wait_ge(ctx_hi_done, j + 1)
                nc.vector.tensor_tensor(ctx_lo[:], ctx_raw[:], ctx_hi[:].bitcast(F32), ALU.subtract).then_inc(ctx_split, 1)

            def input_lo(j):
                dve.wait_ge(in_hi_done, j + 1)
                nc.vector.tensor_tensor(in_lo[:], turned[:], in_hi[:].bitcast(F32), ALU.subtract).then_inc(in_split, 1)

            def hidden_lo(j):
                dve.wait_ge(y_hi_done, j + 1)
                nc.vector.tensor_tensor(y_lo[:], turned[:], y_hi[:].bitcast(F32), ALU.subtract).then_inc(y_split, 1)

            def query_parts(j):
                wait_drained(dve, "Q", j)
                if j > 0:
                    if j == 1:
                        dve.wait_ge(q_copied, 8)
                        dve.wait_ge(q_stacked_pool, 16 * 4)
                    else:
                        dve.wait_ge(q_stacked, 16 * 12 * (j - 1))
                for e in range(2):
                    nc.vector.tensor_scalar(q_hi[:, e], q_raw[:], vec[:, V_PARITY + e:V_PARITY + e + 1], None, ALU.mult).then_inc(q_split, 1)
                dve.wait_ge(q_split, 4 * j + 2)
                for e in range(2):
                    nc.vector.scalar_tensor_tensor(q_lo[:, e], q_raw[:], vec[:, V_PARITY + e:V_PARITY + e + 1],
                                                   q_hi[:, e].bitcast(F32), ALU.mult, ALU.subtract).then_inc(q_split, 1)

            def key_lo(j, s):
                bank = wait_full(dve, "K", j, s)
                dve.wait_ge(k_hi_done, C * (k_bursts_before(j) + s + 1))
                for c in range(C):
                    ins = nc.vector.scalar_tensor_tensor(k_lo[:, s, c, :], bank[:, c * T:c * T + T], col(layer(j), V_KB, c),
                                                         k_hi[:, s, c, :].bitcast(F32), ALU.add, ALU.subtract)
                    ins.then_inc(drained("K", j, s) if c == C - 1 else k_lo_half, 1)

            def maxima(j, b, half):
                n = sources(j)
                for name in score_bursts(j, b, half):
                    bank = wait_full(dve, *name)
                    heads = 4 // n
                    i = name[3]
                    if i == 0 and j > 0:
                        wait_full(dve, "TM", j - 1, b)
                    first = 8 * (i % 2) + i // 2 if n == 1 else 4 * (i % 4) + i // 4
                    nc.vector.tensor_reduce(neg_max[:, b, first:first + 2 * heads - 1:2],
                                            bank[:].rearrange("p (h n) -> p h n", h=heads), AX.X, ALU.max,
                                            negate=True).then_inc(drained(*name), 1)

            def max_rows(j, b):
                bank = wait_full(dve, "TM", j, b)
                if j > 0:
                    dve.wait_ge(max_stacked[b], 16 * j)
                nc.vector.tensor_copy(neg_maxT[:, b, :], bank[0:H, 0:P]).then_inc(drained("TM", j, b), 1)

            def take_heads(j, b):
                dve.wait_ge(o_full, 2 * j + b + 1)
                if j > 0:
                    wait_full(dve, "TO", j - 1, b)
                nc.vector.tensor_copy(o_raw[:, b, :], o_bank[:]).then_inc(o_drained, 1)

            def normalise_heads(j, b):
                bank = wait_full(dve, "TO", j, b)
                by_head = bank[:].rearrange("p (h w) -> p h w", w=32)
                u = 2 * j + b
                if j > 0:
                    wait_full(dve, "TY", j - 1)
                nc.vector.reciprocal(o_recip[:, b, :].rearrange("p (h o) -> p h o", o=1), by_head[:, :, HD:HD + 1]).then_inc(recip_done, 1)
                dve.wait_ge(recip_done, u + 1)
                nc.vector.tensor_tensor(normed[:, b, :].rearrange("p (h d) -> p h d", d=HD), by_head[:, :, 0:HD],
                                        o_recip[:, b, :].rearrange("p (h o) -> p h o", o=1).to_broadcast([P, H, HD]),
                                        ALU.mult).then_inc(drained("TO", j, b), 1)

            def out_lo(j):
                bank = wait_full(dve, "TOT", j)
                dve.wait_ge(oT_hi_done, C * (j + 1))
                for c in range(C):
                    ins = nc.vector.scalar_tensor_tensor(oT_lo[:, c, :], bank[:, c * T:c * T + T], col(layer(j), V_VB, c),
                                                         oT_hi[:, c, :].bitcast(F32), ALU.add, ALU.subtract)
                    ins.then_inc(drained("TOT", j) if c == C - 1 else oT_lo_half, 1)

            def residual(j):
                bank = wait_full(dve, "OUT", j)
                dve.wait_ge(res_base, j + 1)
                nc.vector.tensor_tensor(h_res[:].rearrange("p t n -> p (t n)"), bank[:], h_res[:].rearrange("p t n -> p (t n)"),
                                        ALU.add).then_inc(drained("OUT", j), 1)

            def hidden_moments(j):
                ell = layer(j)
                wait_drained(dve, "OUT", j)
                for t in range(2):
                    link(nc.vector.bn_stats(stats[:, t, :], h_res[:, t, :]))
                for t in range(2):
                    link(nc.vector.bn_aggr(moments[:, t, :], stats[:, t, :]))
                if ell == 0:
                    nc.vector.tensor_scalar(spread[:], moments[:, :, 1], EPS[0], None, ALU.add).then_inc(ln_steps, 1)
                else:
                    link(nc.vector.tensor_tensor(spread[:], moments[:, :, 0], moments[:, :, 0], ALU.mult))
                    link(nc.vector.tensor_tensor(spread[:], spread[:], moments[:, :, 1], ALU.add))
                    nc.vector.tensor_scalar(spread[:], spread[:], EPS[1], None, ALU.add).then_inc(ln_steps, 1)

            def hidden_norm(j):
                dve.wait_ge(rstd_done, j + 1)
                for t in range(2):
                    if layer(j) == 0:
                        ins = nc.vector.tensor_scalar(normed[:, t, :], h_res[:, t, :], moments[:, t, 0:1], rstd[:, t:t + 1],
                                                      ALU.subtract, ALU.mult)
                    else:
                        ins = nc.vector.tensor_scalar(normed[:, t, :], h_res[:, t, :], rstd[:, t:t + 1], None, ALU.mult)
                    ins.then_inc(h_normed, 1)

            def gelu_parts(j, i):
                wait_drained(dve, "H1", j, i)
                n = SLICES * j + i
                if n >= 2:
                    wait_hid_used(dve, n - 2)
                nc.vector.tensor_copy(hid_hi[:, i % 2], gelu_raw[:, i % 2]).then_inc(hid_hi_done, 1)
                dve.wait_ge(hid_hi_done, n + 1)
                nc.vector.tensor_tensor(hid_lo[:, i % 2], gelu_raw[:, i % 2], hid_hi[:, i % 2].bitcast(F32),
                                        ALU.subtract).then_inc(hid_split, 1)

            def finish(j):
                g = j % PAIRS
                dve.wait_ge(mlp_full, j + 1)
                dve.wait_ge(out_base, j + 1)
                xg = x_sb[:, 2 * g:2 * g + 2, :].rearrange("p t n -> p (t n)")
                nc.vector.tensor_tensor(xg, mlp_bank[:], xg, ALU.add).then_inc(mlp_drained, 1)

            nc.vector.memset(v_ones[:], 0.0).then_inc(v_set, 1)
            dve.wait_ge(v_set, 1)
            nc.vector.memset(v_ones[:, :, :, :, HD:HD + 1], 1.0).then_inc(v_set, 1)
            dve.wait_ge(consts_in, 32)
            input_norm(0)
            input_norm_apply(0)
            context_lo(0)
            weights_lo(0, 1)
            input_lo(0)
            weights_lo(1, 3)
            input_norm(1)
            setup_masks()
            input_norm_apply(1)
            query_parts(0)
            key_lo(0, 0)
            dve.wait_ge(q_split, 4)
            for r, part in enumerate((q_hi, q_lo)):
                for p in range(4):
                    nc.vector.tensor_copy(q_stack[32 * r:32 * r + 32, p], part[32 * p:32 * p + 32]).then_inc(q_copied, 1)
            context_lo(1)
            input_lo(1)
            for j in range(JOBS):
                more, two = j + 1 < JOBS, j + 1 < JOBS and sources(j + 1) == 2
                mlp, early = j > 0, not more
                fresh = j + 2 < PAIRS
                maxima(j, 0, 0)
                maxima(j, 0, 1)
                if layer(j) == 1 and not early:
                    gelu_parts(j - 2, 3)
                max_rows(j, 0)
                maxima(j, 1, 0)
                if more and layer(j) == 1:
                    key_lo(j + 1, 0)
                maxima(j, 1, 1)
                if layer(j) == 0:
                    first = two or j < 2
                    if first:
                        key_lo(j + 1, 0)
                    max_rows(j, 1)
                    if not first:
                        key_lo(j + 1, 0)
                if two:
                    key_lo(j + 1, 1)
                if layer(j) == 1:
                    max_rows(j, 1)
                if early:
                    gelu_parts(j - 1, 0)
                    gelu_parts(j - 1, 1)
                if j > 1 and layer(j) == 0:
                    gelu_parts(j - 2, 3)
                if more:
                    query_parts(j + 1)
                if j == 0:
                    weights_lo(3, 6)
                if fresh:
                    input_norm(j + 2)
                take_heads(j, 0)
                if j > 1:
                    finish(j - 2)
                if fresh:
                    input_norm_apply(j + 2)
                if j == 0:
                    weights_lo(6, 3 + W_RING)
                take_heads(j, 1)
                normalise_heads(j, 0)
                if mlp and layer(j) == 1 and not early:
                    gelu_parts(j - 1, 0)
                normalise_heads(j, 1)
                if mlp and layer(j) == 0:
                    gelu_parts(j - 1, 0)
                if mlp and not early:
                    gelu_parts(j - 1, 1)
                out_lo(j)
                if j == 0:
                    weights_lo(3 + W_RING, FIRST_L1)
                residual(j)
                hidden_moments(j)
                if mlp:
                    gelu_parts(j - 1, 2)
                if early:
                    gelu_parts(j - 1, 3)
                hidden_norm(j)
                if j + 2 == JOBS:
                    gelu_parts(j - 1, 3)
                if early:
                    finish(j - 1)
            hidden_lo(JOBS - 1)
            for i in range(SLICES):
                gelu_parts(JOBS - 1, i)
            finish(JOBS - 1)

        @block.gpsimd
        def _(pool):
            def context_lo(j):
                pool.wait_ge(ctx_hi_done, j + 1)
                nc.gpsimd.tensor_tensor(ctx_lo[:], ctx_raw[:], ctx_hi[:].bitcast(F32), ALU.subtract).then_inc(ctx_split, 1)

            def input_lo(j):
                pool.wait_ge(in_hi_done, j + 1)
                nc.gpsimd.tensor_tensor(in_lo[:], turned[:], in_hi[:].bitcast(F32), ALU.subtract).then_inc(in_split, 1)

            def hidden_lo(j):
                pool.wait_ge(y_hi_done, j + 1)
                nc.gpsimd.tensor_tensor(y_lo[:], turned[:], y_hi[:].bitcast(F32), ALU.subtract).then_inc(y_split, 1)

            def input_rstd(j):
                pool.wait_ge(x_moments, 6 * (j + 1))
                nc.gpsimd.tensor_tensor(rstd_in[:], spread_in[:], minus_half[:], ALU.pow).then_inc(x_rstd, 1)

            def residual_base(j):
                g = j % PAIRS
                if j > 0:
                    pool.wait_ge(h_normed, 2 * j)
                    pool.wait_ge(out_base, j)
                if layer(j) == 1:
                    pool.wait_ge(mlp_drained, g + 1)
                else:
                    pool.wait_ge(x_in[g], 16)
                for t in range(2):
                    ins = nc.gpsimd.tensor_tensor(h_res[:, t, :], x_sb[:, 2 * g + t, :], bias_rows[:, 2 * layer(j), :], ALU.add)
                    ins.then_inc(res_base if t else pool_half, 1)

            def hidden_rstd(j):
                pool.wait_ge(ln_steps, j + 1)
                nc.gpsimd.tensor_tensor(rstd[:], spread[:], minus_half[:], ALU.pow).then_inc(rstd_done, 1)

            def output_base(j):
                g = j % PAIRS
                wait_drained(pool, "OUT", j)
                if layer(j) == 1:
                    pool.wait_ge(res_base, j + 1)
                for t in range(2):
                    src = h_res[:, t, :] if layer(j) == 0 else x_sb[:, 2 * g + t, :]
                    ins = nc.gpsimd.tensor_tensor(x_sb[:, 2 * g + t, :], src, bias_rows[:, 2 * layer(j) + 1, :], ALU.add)
                    ins.then_inc(out_base if t else pool_half, 1)

            def weights_lo(first, last):
                for n in range(first, last):
                    pool.wait_ge(w_hi_done, n + 1)
                    s = CHUNK_SLOT[n]
                    nc.gpsimd.tensor_tensor(w_lo[:, s].rearrange("p a b -> p (a b)"), w_raw[:, n % W_RING, :],
                                            w_hi[:, s].rearrange("p a b -> p (a b)").bitcast(F32), ALU.subtract).then_inc(w_lo_pool, 1)

            def stack_latents(j):
                pool.wait_ge(o_full, 2 * j)
                wait_drained(pool, "K", j, 1)
                for r, part in ((1, k_hi), (2, k_lo)):
                    for p in range(4):
                        pool.dma_start(k_stack[32 * r:32 * r + 32, 0, p].bitcast(F32),
                                       part[32 * p:32 * p + 32, 1].bitcast(F32)).then_inc(latents_stacked_pool, 16)

            def stack_max(j, b):
                wait_drained(pool, "TM", j, b)
                dst = q_stack[MAX_ROW:MAX_ROW + 1, :, :, :, b * P:b * P + P].bitcast(F32)
                pool.dma_start(dst.rearrange("o p e c n -> o (p e c) n"),
                             neg_maxT[:, b, :].bitcast(F32)).then_inc(max_stacked[b], 16)

            nc.gpsimd.memset(minus_half[:], -0.5).then_inc(consts_set, 1)
            pool.wait_ge(consts_set, 1)
            nc.gpsimd.memset(q_stack[MASK_ROW:MASK_ROW + 2].bitcast(F32), 1.0).then_inc(ones_set, 1)
            pool.wait_ge(ones_set, 1)
            input_rstd(0)
            pool.wait_ge(x_rstd, 1)
            nc.gpsimd.memset(k_stack[MASK_ROW:MASK_ROW + 2].bitcast(F32), 1.0).then_inc(ones_set, 1)
            pool.wait_ge(ones_set, 2)
            nc.gpsimd.memset(k_stack[MASK_ROW:MASK_ROW + 1, 0].bitcast(F32), 0.0).then_inc(ones_set, 1)
            pool.wait_ge(ones_set, 3)
            input_rstd(1)
            pool.wait_ge(q_split, 4)
            for p in range(4):
                pool.dma_start(q_stack[64:96, p].bitcast(F32), q_hi[32 * p:32 * p + 32].bitcast(F32)).then_inc(q_stacked_pool, 16)
            pool.wait_ge(biases_in, 16)
            for j in range(JOBS):
                if j + 1 == JOBS:
                    hidden_lo(j - 1)
                stack_max(j, 0)
                if j > 0:
                    output_base(j - 1)
                    if j + 1 < JOBS:
                        hidden_lo(j - 1)
                stack_max(j, 1)
                residual_base(j)
                if j + 2 < PAIRS:
                    input_rstd(j + 2)
                if j == 2:
                    weights_lo(FIRST_L1, FIRST_L1_MLP)
                if j == PAIRS + 1:
                    weights_lo(FIRST_L1_MLP, LAST_PROJ)
                if j + 1 < JOBS and layer(j + 1) == 1:
                    stack_latents(j + 1)
                if j == PAIRS + 1:
                    weights_lo(LAST_PROJ, len(CHUNK_SLOT))
                hidden_rstd(j)
                if j + 2 < JOBS:
                    input_lo(j + 2)
                    context_lo(j + 2)
            output_base(JOBS - 1)


def kernel(**inputs):
    import numpy as np
    import concourse.bacc as bacc
    from concourse.bass_utils import run_bass_kernel_spmd

    a = {k: np.asarray(v) for k, v in inputs.items()}
    l0 = lambda n: a["L0_xattn_" + n]
    l1 = lambda n: a["L1_xattn_" + n]

    def square(w):
        return w.reshape(C, P, D).transpose(1, 0, 2).reshape(1, P, C * D)

    def wide(w):
        return w.reshape(C, P, SLICES, D).transpose(2, 1, 0, 3).reshape(SLICES, P, C * D)

    def tall(w):
        return w.reshape(SLICES, 2, P, D).transpose(0, 2, 1, 3).reshape(SLICES, P, 2 * D)

    kv = l1("kv_w").reshape(D, D, 2)
    weights = np.concatenate([square(l0("q_w")), square(l0("k_w")), square(l0("v_w")), square(l0("cproj_w")),
                              np.stack([wide(l0("fc_w")), tall(l0("proj_w"))], axis=1).reshape(2 * SLICES, P, 2 * D),
                              square(l1("q_w")), square(kv[:, :, 0]), square(kv[:, :, 1]), square(l1("out_w")),
                              wide(l1("mlp_w1")), tall(l1("mlp_w2"))])

    def cols(v):
        return v.reshape(-1, P).T

    kvb = l1("kv_b").reshape(D, 2)
    zero, one = np.zeros(D, np.float32), np.ones(D, np.float32)
    head = (np.arange(P) // HD) % 2
    parity = np.stack([head == 0, head == 1], axis=1).astype(np.float32)
    vectors = np.concatenate(
        [cols(v) for v in (l0("ln1_w"), l0("ln1_b"), l0("q_b"), l0("k_b"), l0("v_b"), l0("ln2_w"), l0("ln2_b"), l0("fc_b"))]
        + [cols(v) for v in (one, zero, l1("q_b"), kvb[:, 0], kvb[:, 1], l1("postnorm_w"), zero, l1("mlp_b1"))]
        + [parity], axis=1)
    arrays = {
        "x": a["x"],
        "ctxT": a["ctx_2048"].reshape(PAIRS, T, C, P).transpose(0, 3, 2, 1),
        "weights": weights,
        "vectors": vectors,
        "rows": np.stack([l0("cproj_b"), l0("proj_b"), l1("out_b"), l1("mlp_b2")]),
        "ident": np.eye(P, dtype=np.float32),
        "mask1": a["mask_BxS2_bf1"].view(np.uint8),
        "mask2": a["mask_BxS2_ik0"],
    }
    arrays = {k: np.ascontiguousarray(v) for k, v in arrays.items()}
    nc = bacc.Bacc("TRN2", target_bir_lowering=False, num_devices=1)
    args = [nc.dram_tensor(k, v.shape, mybir.dt.from_np(v.dtype), kind="ExternalInput").ap() for k, v in arrays.items()]
    args.append(nc.dram_tensor("out", (B, P, D), F32, kind="ExternalOutput").ap())
    xattn_kernel(nc, *args)
    r = run_bass_kernel_spmd(nc, [arrays], core_ids=[0])
    return r.results[0]["out"]
```
